# Optimizing a Trainium2 kernel written in Bass

```python
import numpy as np
import jax
import jax.numpy as jnp

def _softmax(x, axis=-1):
    return jax.nn.softmax(x, axis=axis)
def _gelu(x):
    return jax.nn.gelu(x, approximate=True)
def _silu(x):
    return jax.nn.silu(x)
def _sigmoid(x):
    return jax.nn.sigmoid(x)
def _layernorm(x, axis=-1, eps=1e-5):
    m = jnp.mean(x, axis=axis, keepdims=True)
    v = jnp.var(x, axis=axis, keepdims=True)
    return (x - m) / jnp.sqrt(v + eps)
def _scatter_add(tgt, idx, src, axis=0):
    return tgt.at[idx].add(src)
def _segment_sum(src, seg, n):
    return jax.ops.segment_sum(src, seg, n)

kernel_name = 'mk_conv_seq_d2_conv_nchw64_ad644e'

def setup_inputs(seed: int = 0):
    np.random.seed(seed)
    _w = jnp.asarray
    def _rec_inputs():
        import jax
        import jax.numpy as jnp
        _gk = jax.random.key(seed)
        x = 7.22e-05 + 1 * jax.random.normal(jax.random.fold_in(_gk, 1), (8, 64, 128, 128), jnp.float32)
        return x
    x = _rec_inputs()
    def _L0_conv_setup():
        import jax, jax.numpy as jnp
        from jax import lax
        import numpy as np
        D_STATE = 16
        D_CONV = 4
        GN_EPS = 1e-05

        def silu(x):
            return x * jax.nn.sigmoid(x)

        def causal_conv(x, w, b):
            xc = jnp.transpose(x, (0, 2, 1))
            y = lax.conv_general_dilated(xc, w, (1,), [(D_CONV - 1, 0)], feature_group_count=w.shape[0], dimension_numbers=('NCH', 'OIH', 'NCH'))
            y = y + b[None, :, None]
            return jnp.transpose(y, (0, 2, 1))

        def selective_scan(u, delta, A, Bm, Cm, D):

            def step(h, inp):
                u_t, d_t, B_t, C_t = inp
                dA = jnp.exp(d_t[..., None] * A)
                h = dA * h + (d_t * u_t)[..., None] * B_t[:, None, :]
                y = jnp.einsum('bdn,bn->bd', h, C_t)
                return (h, y)
            h0 = jnp.zeros((u.shape[0], A.shape[0], A.shape[1]), u.dtype)
            xs = (jnp.transpose(u, (1, 0, 2)), jnp.transpose(delta, (1, 0, 2)), jnp.transpose(Bm, (1, 0, 2)), jnp.transpose(Cm, (1, 0, 2)))
            _, ys = lax.scan(step, h0, xs)
            return jnp.transpose(ys, (1, 0, 2)) + u * D

        def mamba(seq, p):
            in_w, conv_w, conv_b, xp_w, dt_w, dt_b, A_log, Dp, out_w = p
            di = in_w.shape[0] // 2
            xz = jnp.einsum('blc,ec->ble', seq, in_w)
            x, z = (xz[..., :di], xz[..., di:])
            x = silu(causal_conv(x, conv_w, conv_b))
            xdbl = jnp.einsum('bld,ed->ble', x, xp_w)
            dtr = dt_w.shape[1]
            dt = xdbl[..., :dtr]
            Bm = xdbl[..., dtr:dtr + D_STATE]
            Cm = xdbl[..., dtr + D_STATE:]
            delta = jax.nn.softplus(jnp.einsum('blr,dr->bld', dt, dt_w) + dt_b)
            A = -jnp.exp(A_log)
            y = selective_scan(x, delta, A, Bm, Cm, Dp)
            y = y * silu(z)
            return jnp.einsum('bld,cd->blc', y, out_w)

        def run_bidir(seq, p):
            f = mamba(seq, p)
            r = jnp.flip(mamba(jnp.flip(seq, 1), p), 1)
            return 0.5 * (f + r)

        def _mamba_params(key, c):
            di = 2 * c
            dtr = max(1, -(-c // 16))
            ks = jax.random.split(key, 7)
            in_w = jax.random.normal(ks[0], (2 * di, c), jnp.float32) * 0.02
            conv_w = jax.random.normal(ks[1], (di, 1, D_CONV), jnp.float32) * 0.1
            conv_b = jnp.zeros((di,), jnp.float32)
            xp_w = jax.random.normal(ks[2], (dtr + 2 * D_STATE, di), jnp.float32) * 0.02
            dt_w = jax.random.normal(ks[3], (di, dtr), jnp.float32) * 0.1
            dt_b = jax.random.normal(ks[4], (di,), jnp.float32) * 0.1 - 4.0
            A_log = jnp.log(jnp.broadcast_to(jnp.arange(1.0, D_STATE + 1.0, dtype=jnp.float32), (di, D_STATE)))
            Dp = jnp.ones((di,), jnp.float32)
            out_w = jax.random.normal(ks[5], (c, di), jnp.float32) * 0.02
            return (in_w, conv_w, conv_b, xp_w, dt_w, dt_b, A_log, Dp, out_w)
        key = jax.random.key(seed)
        b, c, h, w = (8, 64, 128, 128)
        kx, kr, kc, kg = jax.random.split(key, 4)
        x = jax.random.normal(kx, (b, c, h, w), jnp.float32)
        rp = _mamba_params(kr, c)
        cp = _mamba_params(kc, c)
        names = ('in_w', 'conv_w', 'conv_b', 'xp_w', 'dt_w', 'dt_b', 'A_log', 'D', 'out_w')
        d = {'x': x}
        for n, v in zip(names, rp):
            d['row_' + n] = v
        for n, v in zip(names, cp):
            d['col_' + n] = v
        d['gn_w'] = jnp.ones((c,), jnp.float32)
        d['gn_b'] = jnp.zeros((c,), jnp.float32)
        return d
    _L0_conv_all = _L0_conv_setup()
    _L0_conv_in = {k: v for k, v in _L0_conv_all.items() if k in ('row_in_w', 'row_conv_w', 'row_conv_b', 'row_xp_w', 'row_dt_w', 'row_dt_b', 'row_A_log', 'row_D', 'row_out_w', 'col_in_w', 'col_conv_w', 'col_conv_b', 'col_xp_w', 'col_dt_w', 'col_dt_b', 'col_A_log', 'col_D', 'col_out_w', 'gn_w', 'gn_b', )}
    del _L0_conv_all

    def _L1_conv_setup():
        import jax, jax.numpy as jnp
        import numpy as np
        from jax import lax
        K = 3

        def _box_mean(x):
            H, W = (x.shape[2], x.shape[3])
            sums = lax.reduce_window(x, 0.0, lax.add, window_dimensions=(1, 1, K, K), window_strides=(1, 1, 1, 1), padding='SAME')
            counts = lax.reduce_window(jnp.ones((H, W), x.dtype), 0.0, lax.add, window_dimensions=(K, K), window_strides=(1, 1), padding='SAME')
            return sums / counts[None, None, :, :]
        key = jax.random.key(seed)
        k1, k2, k3 = jax.random.split(key, 3)
        B, C, H, W = (32, 64, 128, 128)
        x = jax.random.normal(k1, (B, C, H, W), dtype=jnp.float32)
        conv_w = jax.random.normal(k2, (C, C), dtype=jnp.float32) * (1.0 / np.sqrt(C))
        conv_b = jax.random.normal(k3, (C,), dtype=jnp.float32) * 0.01
        return {'x': x, 'conv_w': conv_w, 'conv_b': conv_b}
    _L1_conv_all = _L1_conv_setup()
    _L1_conv_in = {k: v for k, v in _L1_conv_all.items() if k in ('conv_w', 'conv_b', )}
    del _L1_conv_all

    return {
        "x": x,
        "L0_conv_row_in_w": _L0_conv_in["row_in_w"],
        "L0_conv_row_conv_w": _L0_conv_in["row_conv_w"],
        "L0_conv_row_conv_b": _L0_conv_in["row_conv_b"],
        "L0_conv_row_xp_w": _L0_conv_in["row_xp_w"],
        "L0_conv_row_dt_w": _L0_conv_in["row_dt_w"],
        "L0_conv_row_dt_b": _L0_conv_in["row_dt_b"],
        "L0_conv_row_A_log": _L0_conv_in["row_A_log"],
        "L0_conv_row_D": _L0_conv_in["row_D"],
        "L0_conv_row_out_w": _L0_conv_in["row_out_w"],
        "L0_conv_col_in_w": _L0_conv_in["col_in_w"],
        "L0_conv_col_conv_w": _L0_conv_in["col_conv_w"],
        "L0_conv_col_conv_b": _L0_conv_in["col_conv_b"],
        "L0_conv_col_xp_w": _L0_conv_in["col_xp_w"],
        "L0_conv_col_dt_w": _L0_conv_in["col_dt_w"],
        "L0_conv_col_dt_b": _L0_conv_in["col_dt_b"],
        "L0_conv_col_A_log": _L0_conv_in["col_A_log"],
        "L0_conv_col_D": _L0_conv_in["col_D"],
        "L0_conv_col_out_w": _L0_conv_in["col_out_w"],
        "L0_conv_gn_w": _L0_conv_in["gn_w"],
        "L0_conv_gn_b": _L0_conv_in["gn_b"],
        "L1_conv_conv_w": _L1_conv_in["conv_w"],
        "L1_conv_conv_b": _L1_conv_in["conv_b"],
    }

def reference(x, L0_conv_row_in_w, L0_conv_row_conv_w, L0_conv_row_conv_b, L0_conv_row_xp_w, L0_conv_row_dt_w, L0_conv_row_dt_b, L0_conv_row_A_log, L0_conv_row_D, L0_conv_row_out_w, L0_conv_col_in_w, L0_conv_col_conv_w, L0_conv_col_conv_b, L0_conv_col_xp_w, L0_conv_col_dt_w, L0_conv_col_dt_b, L0_conv_col_A_log, L0_conv_col_D, L0_conv_col_out_w, L0_conv_gn_w, L0_conv_gn_b, L1_conv_conv_w, L1_conv_conv_b):
    import jax
    import jax.numpy as jnp
    def _L0_conv_ref(x, row_in_w, row_conv_w, row_conv_b, row_xp_w, row_dt_w, row_dt_b, row_A_log, row_D, row_out_w, col_in_w, col_conv_w, col_conv_b, col_xp_w, col_dt_w, col_dt_b, col_A_log, col_D, col_out_w, gn_w, gn_b):
        import jax, jax.numpy as jnp
        from jax import lax
        import numpy as np
        D_STATE = 16
        D_CONV = 4
        GN_EPS = 1e-05

        def silu(x):
            return x * jax.nn.sigmoid(x)

        def causal_conv(x, w, b):
            xc = jnp.transpose(x, (0, 2, 1))
            y = lax.conv_general_dilated(xc, w, (1,), [(D_CONV - 1, 0)], feature_group_count=w.shape[0], dimension_numbers=('NCH', 'OIH', 'NCH'))
            y = y + b[None, :, None]
            return jnp.transpose(y, (0, 2, 1))

        def selective_scan(u, delta, A, Bm, Cm, D):

            def step(h, inp):
                u_t, d_t, B_t, C_t = inp
                dA = jnp.exp(d_t[..., None] * A)
                h = dA * h + (d_t * u_t)[..., None] * B_t[:, None, :]
                y = jnp.einsum('bdn,bn->bd', h, C_t)
                return (h, y)
            h0 = jnp.zeros((u.shape[0], A.shape[0], A.shape[1]), u.dtype)
            xs = (jnp.transpose(u, (1, 0, 2)), jnp.transpose(delta, (1, 0, 2)), jnp.transpose(Bm, (1, 0, 2)), jnp.transpose(Cm, (1, 0, 2)))
            _, ys = lax.scan(step, h0, xs)
            return jnp.transpose(ys, (1, 0, 2)) + u * D

        def mamba(seq, p):
            in_w, conv_w, conv_b, xp_w, dt_w, dt_b, A_log, Dp, out_w = p
            di = in_w.shape[0] // 2
            xz = jnp.einsum('blc,ec->ble', seq, in_w)
            x, z = (xz[..., :di], xz[..., di:])
            x = silu(causal_conv(x, conv_w, conv_b))
            xdbl = jnp.einsum('bld,ed->ble', x, xp_w)
            dtr = dt_w.shape[1]
            dt = xdbl[..., :dtr]
            Bm = xdbl[..., dtr:dtr + D_STATE]
            Cm = xdbl[..., dtr + D_STATE:]
            delta = jax.nn.softplus(jnp.einsum('blr,dr->bld', dt, dt_w) + dt_b)
            A = -jnp.exp(A_log)
            y = selective_scan(x, delta, A, Bm, Cm, Dp)
            y = y * silu(z)
            return jnp.einsum('bld,cd->blc', y, out_w)

        def run_bidir(seq, p):
            f = mamba(seq, p)
            r = jnp.flip(mamba(jnp.flip(seq, 1), p), 1)
            return 0.5 * (f + r)

        def _mamba_params(key, c):
            di = 2 * c
            dtr = max(1, -(-c // 16))
            ks = jax.random.split(key, 7)
            in_w = jax.random.normal(ks[0], (2 * di, c), jnp.float32) * 0.02
            conv_w = jax.random.normal(ks[1], (di, 1, D_CONV), jnp.float32) * 0.1
            conv_b = jnp.zeros((di,), jnp.float32)
            xp_w = jax.random.normal(ks[2], (dtr + 2 * D_STATE, di), jnp.float32) * 0.02
            dt_w = jax.random.normal(ks[3], (di, dtr), jnp.float32) * 0.1
            dt_b = jax.random.normal(ks[4], (di,), jnp.float32) * 0.1 - 4.0
            A_log = jnp.log(jnp.broadcast_to(jnp.arange(1.0, D_STATE + 1.0, dtype=jnp.float32), (di, D_STATE)))
            Dp = jnp.ones((di,), jnp.float32)
            out_w = jax.random.normal(ks[5], (c, di), jnp.float32) * 0.02
            return (in_w, conv_w, conv_b, xp_w, dt_w, dt_b, A_log, Dp, out_w)
        rp = (row_in_w, row_conv_w, row_conv_b, row_xp_w, row_dt_w, row_dt_b, row_A_log, row_D, row_out_w)
        cp = (col_in_w, col_conv_w, col_conv_b, col_xp_w, col_dt_w, col_dt_b, col_A_log, col_D, col_out_w)
        b, c, h, w = x.shape
        xr = jnp.transpose(x, (0, 2, 3, 1)).reshape(b * h, w, c)
        xr = run_bidir(xr, rp).reshape(b, h, w, c)
        xr = jnp.transpose(xr, (0, 3, 1, 2))
        xc = jnp.transpose(x, (0, 3, 2, 1)).reshape(b * w, h, c)
        xc = run_bidir(xc, cp).reshape(b, w, h, c)
        xc = jnp.transpose(xc, (0, 3, 2, 1))
        x_rec = 0.5 * (xr + xc)
        g = 4
        xg = x_rec.reshape(b, g, c // g, h, w)
        mu = jnp.mean(xg, axis=(2, 3, 4), keepdims=True)
        var = jnp.var(xg, axis=(2, 3, 4), keepdims=True)
        xg = (xg - mu) * lax.rsqrt(var + GN_EPS)
        xn = xg.reshape(b, c, h, w) * gn_w[None, :, None, None] + gn_b[None, :, None, None]
        return silu(xn) + x

    def _L1_conv_ref(x, conv_w, conv_b):
        import jax, jax.numpy as jnp
        import numpy as np
        from jax import lax
        K = 3

        def _box_mean(x):
            H, W = (x.shape[2], x.shape[3])
            sums = lax.reduce_window(x, 0.0, lax.add, window_dimensions=(1, 1, K, K), window_strides=(1, 1, 1, 1), padding='SAME')
            counts = lax.reduce_window(jnp.ones((H, W), x.dtype), 0.0, lax.add, window_dimensions=(K, K), window_strides=(1, 1), padding='SAME')
            return sums / counts[None, None, :, :]
        x_denoised = _box_mean(x)
        y = jnp.einsum('bchw,oc->bohw', x_denoised, conv_w) + conv_b[None, :, None, None]
        return x + y

    def _gn(v, G=32, eps=1e-5):
        B_, C_, H_, W_ = v.shape
        g = v.reshape(B_, G, C_ // G, H_, W_)
        m = jnp.mean(g, axis=(2, 3, 4), keepdims=True)
        s = jnp.var(g, axis=(2, 3, 4), keepdims=True)
        return ((g - m) / jnp.sqrt(s + eps)).reshape(v.shape)

    def _ln_c(v, eps=1e-6):
        m = jnp.mean(v, axis=1, keepdims=True)
        s = jnp.var(v, axis=1, keepdims=True)
        return (v - m) / jnp.sqrt(s + eps)

    def _ln_t(v, eps=1e-5):
        m = jnp.mean(v, axis=-1, keepdims=True)
        s = jnp.var(v, axis=-1, keepdims=True)
        return (v - m) / jnp.sqrt(s + eps)

    def _to_tokens(v):
        B_, C_, H_, W_ = v.shape
        return v.reshape(B_, C_, H_ * W_).transpose(0, 2, 1)
    def _from_tokens(t, like):
        B_, C_, H_, W_ = like.shape
        return t.transpose(0, 2, 1).reshape(B_, C_, H_, W_)

    x = _L0_conv_ref(x, L0_conv_row_in_w, L0_conv_row_conv_w, L0_conv_row_conv_b, L0_conv_row_xp_w, L0_conv_row_dt_w, L0_conv_row_dt_b, L0_conv_row_A_log, L0_conv_row_D, L0_conv_row_out_w, L0_conv_col_in_w, L0_conv_col_conv_w, L0_conv_col_conv_b, L0_conv_col_xp_w, L0_conv_col_dt_w, L0_conv_col_dt_b, L0_conv_col_A_log, L0_conv_col_D, L0_conv_col_out_w, L0_conv_gn_w, L0_conv_gn_b)
    x = _L1_conv_ref(x, L1_conv_conv_w, L1_conv_conv_b)
    return x


_drawn_inputs = setup_inputs


def setup_inputs(seed=0):
    import zlib

    import numpy as np

    out = dict(_drawn_inputs(seed))
    spreads = {'L0_conv_row_conv_b': (0.0, 0.1),
     'L0_conv_row_D': (1.0, 0.6),
     'L0_conv_col_conv_b': (0.0, 0.1),
     'L0_conv_col_D': (1.0, 0.6),
     'L0_conv_gn_w': (1.0, 0.6),
     'L0_conv_gn_b': (0.0, 0.1)}
    factors = {'L0_conv_row_conv_w': 2.97,
     'L0_conv_row_xp_w': 8.0,
     'L0_conv_row_dt_w': 8.0,
     'L0_conv_row_dt_b': 8.0,
     'L0_conv_row_A_log': 8.0,
     'L0_conv_col_conv_w': 2.849,
     'L0_conv_col_xp_w': 8.0,
     'L0_conv_col_dt_w': 8.0,
     'L0_conv_col_dt_b': 8.0,
     'L0_conv_col_A_log': 8.0,
     'L1_conv_conv_b': 6.346}
    for name, (base, spread) in spreads.items():
        noise = np.random.default_rng([zlib.crc32(name.encode()), seed]).standard_normal(out[name].shape)
        drawn = base * np.exp(spread * noise) if base else spread * noise
        out[name] = jnp.asarray(drawn.astype(out[name].dtype))
    for name, factor in factors.items():
        out[name] = (out[name] * factor).astype(out[name].dtype)
    return out
```

```python
from contextlib import ExitStack

import concourse.bass as bass
from concourse import mybir

ALU = mybir.AluOpType
ACT = mybir.ActivationFunctionType
F32 = mybir.dt.float32
BF16 = mybir.dt.bfloat16

P = 128
TAPS = 4
STATES = 16
SEQS = 4
UNITS = 16
SUMS = UNITS // 2
BC_SLOTS = (10, 12, 13, 14)
SILU_FLOOR = -44.0
GN_GROUPS = 4
GN_EPS = 1e-5


def unit_parts(unit):
    return (unit // 2) % 2, unit // 4, (2 * (unit % 2), 2 * (unit % 2) + 1)


def build(nc, x, inT, convT, xpT, xpdt, dtT, alog, chan, outT, gn, mixT, eye, sel, statesum, groupmean, out):
    B, C, H, W = x.shape
    DI = 2 * C
    L = W
    TOK = SEQS * L
    TILES = H // SEQS
    PER_IMAGE = 2 * TILES
    HALF = H // 2
    PIX = HALF * W
    S = W + TAPS - 1
    PAD = TAPS - 1
    XP = (H + 2 * PAD) * S + PAD
    GW = W + 2
    GR = HALF + 2
    HS_AT = GR * GW
    assert H == W == P and DI == P and HS_AT + GR * W <= XP

    with ExitStack() as ctx:
        def sb(name, shape, dt=F32):
            return ctx.enter_context(nc.sbuf_tensor(name, shape, dt))

        def sem(name):
            return ctx.enter_context(nc.semaphore(name))

        xp = sb("xp", [P, XP])
        xrec = sb("xrec", [P, PIX])
        u = sb("u", [P, 2, TOK])
        delta = sb("delta", [P, 2, TOK])
        parts = sb("parts", [P, 3, 2, 2 * TOK], BF16)
        ring = sb("ring", [3 * 32, 2, 2, 2 * TOK], BF16)
        Bb = sb("Bb", [P, 2, 2, TOK])
        Cb = sb("Cb", [P, 2, 2, TOK])
        tmp0 = sb("tmp0", [P, 2, TOK])
        tmp1 = sb("tmp1", [P, 2, TOK])
        tmp2 = sb("tmp2", [P, 2, TOK])
        decay = sb("decay", [P, 2, 2, SEQS, L])
        hid = sb("hid", [P, 2, 2, TOK])
        hc = sb("hc", [P, 4, 2, TOK])
        zs = sb("zs", [P, 2, TOK])
        yg = sb("yg", [P, TOK])
        conv_w = sb("conv_w", [P, 2, 4, P])
        z_w = sb("z_w", [P, 2, P])
        dt_w = sb("dt_w", [P, 2, P])
        B_w = sb("B_w", [P, 2, P])
        C_w = sb("C_w", [P, 2, P])
        D_w = sb("D_w", [P, 2, P])
        out_w = sb("out_w", [P, 2, C])
        A_s = sb("A_s", [P, 2, STATES])
        chan_s = sb("chan_s", [P, 2, 3])
        gn_s = sb("gn_s", [P, 3])
        sel_s = sb("sel_s", [3 * 32, 4, P], BF16)
        sum_s = sb("sum_s", [P, 4, 32])
        mean_s = sb("mean_s", [P, P])
        mix_s = sb("mix_s", [P, P])
        stats = sb("stats", [P, PIX // 512, 6])
        st = sb("st", [P, 16])

        pd = ctx.enter_context(nc.psum_tensor("pd", [P, 2, 2, 512], F32))
        pu = ctx.enter_context(nc.psum_tensor("pu", [P, 2, 512], F32))
        py = ctx.enter_context(nc.psum_tensor("py", [P, 512], F32))
        pre = ctx.enter_context(nc.psum_tensor("pre", [P, 512], F32))

        loaded = sem("weights_loaded")
        w_dve = sem("weights_made")
        w_exp = sem("a_exp_done")
        w_pe = sem("dt_product_ready")
        x_loaded = sem("x_loaded")
        pads_ready = sem("pads_ready")
        delta_ready = sem("delta_ready")
        du_ready = sem("du_ready")
        hc_used = sem("hc_used")
        conv_ready = sem("conv_ready")
        z_ready = sem("z_ready")
        dpre_ready = sem("dpre_ready")
        bc_ready = sem("bc_ready")
        out_ready = sem("out_ready")
        skip_done = sem("skip_done")
        ring_loaded = [[sem(f"ring_loaded_{t}_{k}") for k in range(2)] for t in ("delta", "du")]
        exp_done = sem("exp_done")
        silu_step = sem("silu_step")
        z_step = sem("z_step")
        dpre_read = sem("dpre_read")
        sp_step = sem("sp_step")
        split_step = sem("split_step")
        bc_read = sem("bc_read")
        mulb_done = sem("mulb_done")
        scan_done = sem("scan_done")
        conv_read = sem("conv_read")
        z_read = sem("z_read")
        u_ready = sem("u_ready")
        zs_ready = sem("zs_ready")
        gate_done = sem("gate_done")
        corr_done = sem("corr_done")
        log_done = sem("log_done")
        delta_made = sem("delta_made")
        du_made = sem("du_made")
        drest_done = sem("drest_done")
        dparts_ready = sem("dparts_ready")
        xrec_done = sem("xrec_done")
        mulc_done = sem("mulc_done")
        urest_done = sem("urest_done")
        uparts_ready = sem("uparts_ready")
        g_loaded = sem("g_loaded")
        stat_done = sem("stat_done")
        gm_ready = sem("gm_ready")
        rstd_step = sem("rstd_step")
        norm_done = sem("norm_done")
        floor_done = sem("floor_done")
        gate_step = sem("gate_step")
        act_done = sem("act_done")
        g_done = sem("g_done")
        halo_loaded = sem("halo_loaded")
        edge_done = sem("edge_done")
        rows_step = sem("rows_step")
        rows_done = sem("rows_done")
        mix_ready = sem("mix_ready")
        final_done = sem("final_done")
        stored = sem("stored")

        ST = 1088

        def scratch(o, at, n):
            return xrec[:, o * ST + at:o * ST + at + n]
        in_t = [scratch(o, 0, 256) for o in range(2)]
        cw_t = [scratch(o, 256, 512) for o in range(2)]
        xp_t = [scratch(o, 768, 36) for o in range(2)]
        al_t = [scratch(o, 804, 16) for o in range(2)]
        xd_t = [scratch(o, 820, P) for o in range(2)]
        dt_t = [scratch(o, 948, P) for o in range(2)]
        eye_t = xrec[:, 2 * ST:2 * ST + P]
        mix_t = xrec[:, 2 * ST + P:2 * ST + 2 * P]
        sel_t = xrec[0:3 * 32, 2 * ST + 2 * P:2 * ST + 6 * P]

        def window(o, i, odd, shift):
            if o == 0:
                at = (i * SEQS + (HALF if odd else 0) + PAD) * S + PAD + shift
                return xp[:, bass.ds(at, SEQS * S)].rearrange("p (s w) -> p s w", w=S)[:, :, 0:L]
            at = i * 2 * SEQS + (SEQS if odd else 0) + PAD + (PAD + shift) * S
            return xp[:, bass.ds(at, L * S)].rearrange("p (t w) -> p w t", w=S)[:, 0:SEQS, :]

        def tokens(ap, backward):
            a = ap.rearrange("p (s t) -> p s t", s=SEQS)
            return a[:, :, L - 1::-1] if backward else a

        g_all = xp[:, 0:GR * GW].rearrange("p (r w) -> p r w", w=GW)
        rows_all = xp[:, HS_AT:HS_AT + GR * W].rearrange("p (r w) -> p r w", w=W)
        sig_all = xp[:, HS_AT:HS_AT + PIX]
        CH = PIX // 8
        CR = CH // W

        def chunk(ap, c):
            return ap[:, c * CH:(c + 1) * CH]

        def g_chunk(c):
            return g_all[:, 1 + c * CR:1 + (c + 1) * CR, 1:1 + W]

        def phases(eng, start, body, flush):
            with eng.Fori(0, B) as b:
                for o in range(2):
                    n0 = b * PER_IMAGE + o * TILES
                    start(b, o, n0)
                    body(o, 0, n0, 0, True, False)
                    with eng.Fori(0, TILES // 2 - 1) as k:
                        body(o, k, n0 + 2 * k + 1, 1, False, False)
                        body(o, k + 1, n0 + 2 * k + 2, 0, False, False)
                    body(o, TILES // 2 - 1, n0 + TILES - 1, 1, False, True)
                    flush(b, o, n0 + TILES - 1)
                    if o == 1:
                        yield b

        block = ctx.enter_context(nc.Block())

        @block.sync
        def _(sp):
            for o in range(2):
                for h in range(2):
                    sp.dma_start(in_t[o][C * h:C * h + C, :], inT[o]).then_inc(loaded, 16)
                sp.dma_start(cw_t[o], convT[o].partition_broadcast(P)).then_inc(loaded, 16)
                sp.dma_start(xp_t[o], xpT[o]).then_inc(loaded, 16)
                sp.dma_start(al_t[o], alog[o]).then_inc(loaded, 16)
                sp.dma_start(xd_t[o][0:4, :], xpdt[o]).then_inc(loaded, 16)
                sp.dma_start(dt_t[o][0:4, :], dtT[o]).then_inc(loaded, 16)
                sp.dma_start(chan_s[:, o, :], chan[o]).then_inc(loaded, 16)
                sp.dma_start(out_w[:, o, :], outT[o]).then_inc(loaded, 16)
            for h in range(2):
                sp.dma_start(gn_s[C * h:C * h + C, :], gn).then_inc(loaded, 16)
                sp.dma_start(mix_t[C * h:C * h + C, 0:C], mixT).then_inc(loaded, 16)
            sp.dma_start(eye_t, eye).then_inc(loaded, 16)
            sp.dma_start(sel_t, sel).then_inc(loaded, 16)
            sp.dma_start(sum_s[:].rearrange("p j m -> p (j m)"), statesum).then_inc(loaded, 16)
            sp.dma_start(mean_s[:], groupmean).then_inc(loaded, 16)

            def interior(lo, shift):
                at = PAD * S + PAD - shift
                a = xp[lo:lo + C, at:at + H * S].rearrange("p (r w) -> p r w", w=S)
                return a[:, :, 0:W]

            def load_ring(n, first):
                for j in range(4):
                    if j > (1 if first else 0):
                        sp.wait_ge(du_ready, n * UNITS + 4 * j - 4)
                    for t in range(2):
                        if j == 0:
                            sp.wait_ge((dparts_ready, uparts_ready)[t], n + 1)
                        for k in range(3):
                            sp.dma_start(ring[32 * k:32 * k + 32, j % 2, t, :],
                                         parts[32 * j:32 * j + 32, k, t, :]).then_inc(ring_loaded[t][j % 2], 16)

            def tiles(n0):
                load_ring(n0, True)
                with sp.Fori(1, TILES) as i:
                    load_ring(n0 + i, False)

            with sp.Fori(0, B) as b:
                image = x[bass.ds(b, 1)].rearrange("a c h w -> (a c) h w")
                pads = sp.snap(b * 2 + 1)
                sp.wait_ge(final_done, b * 16)
                sp.wait_ge(pads_ready, pads)
                sp.dma_start(interior(0, 0), image).then_inc(x_loaded, 16)
                sp.dma_start(interior(C, 1), image).then_inc(x_loaded, 16)
                tiles(b * PER_IMAGE)
                sp.wait_ge(z_ready, b * PER_IMAGE + TILES)
                sp.dma_start(interior(C, S), image).then_inc(x_loaded, 16)
                tiles(b * PER_IMAGE + TILES)
                sp.wait_ge(z_ready, b * PER_IMAGE + PER_IMAGE)
                for h in range(2):
                    sp.dma_start(g_all[C * h:C * h + C, 1:1 + HALF, 1:1 + W],
                                 image[:, HALF * h:HALF * h + HALF, :]).then_inc(g_loaded, 16)
                sp.wait_ge(g_done, b * 8 + 8)
                sp.dma_start(g_all[0:C, GR - 1, 1:1 + W], g_all[C:P, 1, 1:1 + W]).then_inc(halo_loaded, 16)
                sp.dma_start(g_all[C:P, 0, 1:1 + W], g_all[0:C, GR - 2, 1:1 + W]).then_inc(halo_loaded, 16)
                result = out[bass.ds(b, 1)].rearrange("a c h w -> (a c) (h w)")
                for c in range(4):
                    sp.wait_ge(final_done, b * 16 + 4 * c + 4)
                    for h in range(2):
                        sp.dma_start(result[:, h * PIX + c * (PIX // 4):h * PIX + (c + 1) * (PIX // 4)],
                                     xrec[C * h:C * h + C, c * (PIX // 4):(c + 1) * (PIX // 4)]
                                     ).then_inc(stored, 16)
            sp.wait_ge(stored, B * 128)

        N_LOADS = 2 * 9 + 4 + 4

        @block.tensor
        def _(pe):
            pe.wait_ge(loaded, 16 * N_LOADS)
            for o in range(2):
                if o == 1:
                    pe.wait_ge(w_dve, 1)
                pe.matmul(pre[:, 0:P], xd_t[o][0:4, :], dt_t[o][0:4, :], start=True, stop=True).then_inc(w_pe, 1)
            pe.wait_ge(w_dve, 3)

            def conv(o, i, odd, m, direction):
                w = conv_w[:, o, 2 * direction:2 * direction + 2, :]
                first, second = ((-3, -1), (0, 2))[direction]
                pe.matmul(pre[:, :], w[:, 0, :], window(o, i, odd, first), start=True, stop=False)
                pe.matmul(pre[:, :], w[:, 1, :], window(o, i, odd, second),
                          start=False, stop=True).then_inc(conv_ready, 1)

            def fill_z(o, i, odd, m):
                pe.wait_ge(conv_read, m * 2 + 2)
                pe.matmul(pre[:, :], z_w[:, o, :], window(o, i, odd, 0), start=True, stop=True).then_inc(z_ready, 1)

            def fill_dpre(o, m, direction):
                if direction:
                    pe.wait_ge(dpre_read, m * 2 + 1)
                pe.matmul(pre[:, :], dt_w[:, o, :], u[:, direction, :],
                          start=True, stop=True).then_inc(dpre_ready, 1)

            def fill_bc(o, m, k):
                if k == 0:
                    pe.wait_ge(dpre_read, m * 2 + 2)
                else:
                    pe.wait_ge(bc_read, m * 4 + k)
                pe.matmul(pre[:, :], (B_w, C_w)[k // 2][:, o, :], u[:, k % 2, :],
                          start=True, stop=True).then_inc(bc_ready, 1)

            def spread_one(n, unit, tensor, banks, ready):
                d, j, quads = unit_parts(unit)
                if unit % 4 == 0:
                    pe.wait_ge(ring_loaded[tensor][j % 2], n * 96 + 48 * (j // 2) + 48)
                for k, q in enumerate(quads):
                    mm = pe.matmul(banks[:, k, :], sel_s[:, q, :], ring[:, j % 2, tensor, d * TOK:(d + 1) * TOK],
                                   start=True, stop=True)
                mm.then_inc(ready, 1)

            def spread(n, unit, with_delta, with_du, first):
                if with_delta:
                    if not (first and unit < 2):
                        pe.wait_ge(exp_done, n * UNITS + unit - 1)
                    spread_one(n, unit, 0, pd[:, unit % 2], delta_ready)
                if with_du:
                    if not (first and unit == 1):
                        pe.wait_ge(mulb_done, n * UNITS + unit - 1)
                    if unit == 0:
                        spread_one(n - 1, UNITS - 1, 1, pu, du_ready)
                    else:
                        spread_one(n, unit - 1, 1, pu, du_ready)

            def state_sum(n, c):
                d, j = c % 2, c // 2
                pe.wait_ge(mulc_done, n * UNITS + 2 * c + 2)
                for q in range(4):
                    mm = pe.matmul(py[32 * q:32 * q + 32, :], sum_s[:, j, :],
                                   tokens(hc[:, (2 * c + q // 2) % 4, q % 2, :], d),
                                   start=False, stop=(c == SUMS - 1), skip_group_check=True)
                mm.then_inc(hc_used, 1)

            def skip_term(o, n, first):
                if not first:
                    pe.wait_ge(gate_done, n)
                pe.matmul(py[:, :], D_w[:, o, :], u[:, 0, :], start=True, stop=False, skip_group_check=True)
                pe.matmul(py[:, :], D_w[:, o, :], tokens(u[:, 1, :], 1), start=False, stop=False,
                          skip_group_check=True).then_inc(skip_done, 1)

            def fill_out(o, m, odd):
                pe.wait_ge(gate_done, m + 1)
                if o == 0:
                    pe.matmul(pre[C * odd:C * odd + C, :], out_w[:, o, :], yg[:, :],
                              start=True, stop=True).then_inc(out_ready, 1)
                else:
                    v = yg[:, :].rearrange("p (s t) -> p s t", s=SEQS)
                    for h in range(2):
                        mm = pe.matmul(pre[C * h:C * h + C, 0:SEQS * HALF], out_w[:, o, :],
                                       v[:, :, HALF * h:HALF * h + HALF], start=True, stop=True)
                    mm.then_inc(out_ready, 1)

            def start(b, o, n0):
                pe.wait_ge(x_loaded, b * 48 + (32 if o == 0 else 48))
                pe.wait_ge(pads_ready, b * 2 + o + 1)
                pe.wait_ge(xrec_done, n0)
                conv(o, 0, 0, n0, 0)
                pe.wait_ge(conv_read, n0 * 2 + 1)
                conv(o, 0, 0, n0, 1)
                fill_z(o, 0, 0, n0)
                pe.wait_ge(z_read, n0 + 1)
                pe.wait_ge(u_ready, n0 + 1)
                for d in range(2):
                    fill_dpre(o, n0, d)
                for k in range(4):
                    fill_bc(o, n0, k)

            def body(o, k, n, par, first, last):
                m, mpar, mi = n + 1, 1 - par, (k + 1 if par else k)
                for s in range(UNITS):
                    spread(n, s, True, not (first and s == 0), first)
                    if not first:
                        if s == 1:
                            state_sum(n - 1, SUMS - 2)
                        if s == 3:
                            state_sum(n - 1, SUMS - 1)
                        if s == 6:
                            if last:
                                pe.wait_ge(bc_read, n * 4 + 4)
                            else:
                                pe.wait_ge(z_read, m + 1)
                            fill_out(o, n - 1, 1 - par)
                    if not last:
                        if s == 0:
                            pe.wait_ge(bc_read, n * 4 + 4)
                            conv(o, mi, mpar, m, 0)
                        if s == 2:
                            pe.wait_ge(conv_read, m * 2 + 1)
                            conv(o, mi, mpar, m, 1)
                        if s == 4:
                            fill_z(o, mi, mpar, m)
                        if s == 7:
                            if first:
                                pe.wait_ge(z_read, m + 1)
                            else:
                                pe.wait_ge(xrec_done, n)
                            pe.wait_ge(u_ready, m + 1)
                            fill_dpre(o, m, 0)
                        if s == 8:
                            fill_dpre(o, m, 1)
                        if s in BC_SLOTS:
                            fill_bc(o, m, BC_SLOTS.index(s))
                    if s == 5:
                        skip_term(o, n, first)
                    if s % 2 and s >= 5:
                        state_sum(n, (s - 5) // 2)

            def flush(b, o, n):
                spread(n + 1, 0, False, True, False)
                state_sum(n, SUMS - 2)
                state_sum(n, SUMS - 1)
                pe.wait_ge(xrec_done, n)
                fill_out(o, n, 1)

            for b in phases(pe, start, body, flush):
                pe.wait_ge(stat_done, b * 10 + 3)
                pe.matmul(pre[:, 0:2], mean_s[:], st[:, 0:2], start=True, stop=True).then_inc(gm_ready, 1)
                for c in range(PIX // 512):
                    if c % 4 == 0:
                        pe.wait_ge(rows_done, b * 4 + c // 4 + 1)
                    if c >= 4:
                        pe.wait_ge(final_done, b * 16 + c - 3)
                    for r in range(3):
                        mm = pe.matmul(pd[:, (c // 2) % 2, c % 2, :], mix_s[:],
                                       rows_all[:, SEQS * c + r:SEQS * c + r + SEQS, :],
                                       start=(r == 0), stop=(r == 2))
                    mm.then_inc(mix_ready, 1)

        @block.scalar
        def _(act):
            act.preload_act_table_set("natural_log_exp_and_others")
            act.wait_ge(loaded, 16 * N_LOADS)
            for o in range(2):
                act.activation(A_s[:, o, :], al_t[o], ACT.Exp).then_inc(w_exp, 1)
            act.wait_ge(w_dve, 3)

            def exps(o, n, unit, first):
                _, j, quads = unit_parts(unit)
                act.wait_ge(delta_ready, n * UNITS + unit + 1)
                if not (first and unit < 2):
                    act.wait_ge(scan_done, n * UNITS + unit - 1)
                for k, q in enumerate(quads):
                    v = pd[:, unit % 2, k, :].rearrange("p (s t) -> p s t", s=SEQS)
                    ins = act.activation(decay[:, unit % 2, k, :, 1:L], v[:, :, 1:L], ACT.Exp,
                                         scale=A_s[:, o, 4 * j + q:4 * j + q + 1])
                ins.then_inc(exp_done, 1)

            def silu_sigmoid(m, step):
                t0, t1 = tmp0[:].rearrange("p d t -> p (d t)"), tmp1[:].rearrange("p d t -> p (d t)")
                if step == 0:
                    act.wait_ge(conv_read, m * 2 + 2)
                    act.activation(t1, t0, ACT.Exp, scale=-1.0).then_inc(silu_step, 1)
                elif step == 1:
                    act.wait_ge(silu_step, m * 3 + 1)
                    act.activation(t1, t1, ACT.Ln, bias=1.0).then_inc(silu_step, 1)
                else:
                    act.wait_ge(silu_step, m * 3 + 2)
                    act.activation(t1, t1, ACT.Exp, scale=-1.0).then_inc(silu_step, 1)

            def z_sigmoid(m, step):
                zin, zout = tmp2[:, 0, :], tmp2[:, 1, :]
                if step == 0:
                    act.wait_ge(z_read, m + 1)
                    act.activation(zout, zin, ACT.Exp, scale=-1.0).then_inc(z_step, 1)
                elif step == 1:
                    act.wait_ge(z_step, m * 3 + 1)
                    act.activation(zout, zout, ACT.Ln, bias=1.0).then_inc(z_step, 1)
                else:
                    act.wait_ge(z_step, m * 3 + 2)
                    act.activation(zout, zout, ACT.Exp, scale=-1.0).then_inc(z_step, 1)

            def read_dpre(o, m, d):
                act.wait_ge(dpre_ready, m * 2 + d + 1)
                act.activation(tmp0[:, d, :], pre[:, :], ACT.Abs, bias=chan_s[:, o, 1:2])
                act.activation(delta[:, d, :], pre[:, :], ACT.Relu, bias=chan_s[:, o, 1:2]).then_inc(dpre_read, 1)

            def softplus(m, step):
                t0, t1, t2 = (t[:].rearrange("p d t -> p (d t)") for t in (tmp0, tmp1, tmp2))
                if step == 0:
                    act.wait_ge(dpre_read, m * 2 + 2)
                    act.activation(t0, t0, ACT.Exp, scale=-1.0).then_inc(sp_step, 1)
                elif step == 1:
                    act.wait_ge(sp_step, m * 3 + 1)
                    act.activation(t1, t0, ACT.Ln, bias=1.0).then_inc(sp_step, 1)
                else:
                    act.wait_ge(zs_ready, m + 1)
                    act.activation(t2, t0, ACT.Identity, bias=1.0).then_inc(sp_step, 1)

            def split(m, step):
                part, tensor = divmod(step, 2)
                if step == 0:
                    for t in range(2):
                        for k in range(2):
                            act.wait_ge(ring_loaded[t][k], m * 96)
                    act.wait_ge(delta_made, m + 1)
                elif step == 1:
                    act.wait_ge(du_made, m + 1)
                else:
                    act.wait_ge((drest_done, urest_done)[tensor], m + 1)
                whole = ((delta, tmp1), (tmp2, tmp0))[part][tensor]
                act.activation(parts[:, part, tensor, :], whole[:].rearrange("p d t -> p (d t)"),
                               ACT.Copy).then_inc(split_step, 1)

            def read_bc(m, par, k):
                act.wait_ge(bc_ready, m * 4 + k + 1)
                act.activation((Bb, Cb)[k // 2][:, par, k % 2, :], pre[:, :], ACT.Copy).then_inc(bc_read, 1)

            def start(b, o, n0):
                act.wait_ge(xrec_done, n0)
                for step in range(3):
                    silu_sigmoid(n0, step)
                for step in range(3):
                    z_sigmoid(n0, step)
                for d in range(2):
                    read_dpre(o, n0, d)
                for step in range(3):
                    softplus(n0, step)
                for step in range(4):
                    split(n0, step)
                for k in range(4):
                    read_bc(n0, 0, k)

            def body(o, k, n, par, first, last):
                m, mpar = n + 1, 1 - par
                for s in range(UNITS):
                    exps(o, n, s, first)
                    if last:
                        continue
                    if 3 <= s <= 5:
                        silu_sigmoid(m, s - 3)
                    if s == 6:
                        z_sigmoid(m, 0)
                        z_sigmoid(m, 1)
                    if s == 7:
                        z_sigmoid(m, 2)
                        read_dpre(o, m, 0)
                    if s == 8:
                        read_dpre(o, m, 1)
                        softplus(m, 0)
                    if s == 9:
                        softplus(m, 1)
                        softplus(m, 2)
                    if s == 12:
                        split(m, 0)
                        split(m, 1)
                    if s == 13:
                        split(m, 2)
                    if s == 14:
                        split(m, 3)
                    if s in BC_SLOTS:
                        read_bc(m, mpar, BC_SLOTS.index(s))

            for b in phases(act, start, body, lambda b, o, n: None):
                act.wait_ge(stat_done, b * 10 + 7)
                act.activation(st[:, 6:7], st[:, 5:6], ACT.Ln).then_inc(rstd_step, 1)
                act.wait_ge(rstd_step, b * 2 + 1)
                act.activation(st[:, 7:8], st[:, 6:7], ACT.Exp, scale=-0.5).then_inc(rstd_step, 1)
                act.wait_ge(stat_done, b * 10 + 10)
                for c in range(8):
                    act.activation(chunk(xrec, c), chunk(xrec, c), ACT.Identity, bias=st[:, 10:11],
                                   scale=st[:, 8:9]).then_inc(norm_done, 1)
                for c in range(8):
                    t = chunk(sig_all, c)
                    act.wait_ge(floor_done, b * 8 + c + 1)
                    act.activation(t, chunk(xrec, c), ACT.Exp, scale=-1.0).then_inc(gate_step, 1)
                    act.wait_ge(gate_step, b * 24 + 3 * c + 1)
                    act.activation(t, t, ACT.Ln, bias=1.0).then_inc(gate_step, 1)
                    act.wait_ge(gate_step, b * 24 + 3 * c + 2)
                    act.activation(t, t, ACT.Exp, scale=-1.0).then_inc(gate_step, 1)

        @block.vector
        def _(dve):
            dve.memset(decay[:], 0.0)
            dve.memset(z_w[:], 0.0)
            dve.memset(mix_s[:], 0.0).then_inc(edge_done, 1)
            dve.wait_ge(edge_done, 1)
            dve.wait_ge(loaded, 16 * N_LOADS)
            for o in range(2):
                for m, (lower, upper) in enumerate(((0, 1), (2, 3), (3, 2), (1, 0))):
                    for h, tap in ((0, lower), (1, upper)):
                        r = slice(C * h, C * h + C)
                        dve.tensor_tensor(conv_w[r, o, m, :], in_t[o][r, 0:P], cw_t[o][r, tap * P:tap * P + P], ALU.mult)
                dve.tensor_copy(z_w[0:C, o, :], in_t[o][0:C, P:2 * P])
                for w, at in ((B_w, 4), (C_w, 4 + STATES)):
                    dve.tensor_copy(w[:, o, :].rearrange("p (c n) -> p c n", n=STATES),
                                    xp_t[o][:, at:at + STATES].unsqueeze(1).to_broadcast([P, P // STATES, STATES]))
                dve.tensor_scalar(D_w[:, o, :], eye_t, chan_s[:, o, 2:3], None, ALU.mult)
                dve.tensor_scalar(out_w[:, o, :], out_w[:, o, :], 0.25, None, ALU.mult)
                dve.wait_ge(w_exp, o + 1)
                dve.tensor_scalar(A_s[:, o, :], A_s[:, o, :], -1.0, None, ALU.mult)
                dve.wait_ge(w_pe, o + 1)
                dve.tensor_copy(dt_w[:, o, :], pre[:, 0:P]).then_inc(w_dve, 1)
            dve.tensor_copy(sel_s[:].rearrange("p j m -> p (j m)"), sel_t)
            for h in range(2):
                r = slice(C * h, C * h + C)
                ins = dve.tensor_scalar(mix_s[r, C * h:C * h + C], mix_t[r, 0:C], 1.0 / 9.0, None, ALU.mult)
            ins.then_inc(w_dve, 1)
            dve.wait_ge(w_dve, 3)

            def mulb(n, par, unit, first):
                d = unit_parts(unit)[0]
                if unit == 0:
                    dve.wait_ge(bc_read, n * 4 + 4)
                dve.wait_ge(du_ready, n * UNITS + unit + 1)
                if not (first and unit < 2):
                    dve.wait_ge(mulc_done, n * UNITS + unit - 1)
                dve.tensor_tensor(hid[:, unit % 2, :, :], pu[:, :, :],
                                  Bb[:, par, d, :].unsqueeze(1).to_broadcast([P, 2, TOK]), ALU.mult).then_inc(mulb_done, 1)

            def scan(n, unit):
                dve.wait_ge(exp_done, n * UNITS + unit + 1)
                dve.wait_ge(mulb_done, n * UNITS + unit + 1)
                h = hid[:, unit % 2, :, :].rearrange("p g t -> p (g t)")
                dve.tensor_tensor_scan(h, decay[:, unit % 2].rearrange("p g s t -> p (g s t)"), h, 0.0,
                                       ALU.mult, ALU.add).then_inc(scan_done, 1)

            def read_conv(o, m, d):
                dve.wait_ge(conv_ready, m * 2 + d + 1)
                dve.wait_ge(uparts_ready, m)
                dve.tensor_scalar(tokens(tmp0[:, d, :], 0), tokens(pre[:, :], d), chan_s[:, o, 0:1], SILU_FLOOR, ALU.add,
                                  ALU.max).then_inc(conv_read, 1)

            def read_z(m):
                dve.wait_ge(z_ready, m + 1)
                dve.tensor_scalar(tmp2[:, 0, :], pre[:, :], SILU_FLOOR, None, ALU.max).then_inc(z_read, 1)

            def silu_u(m):
                dve.wait_ge(silu_step, m * 3 + 3)
                dve.wait_ge(skip_done, m)
                dve.tensor_tensor(u[:], tmp0[:], tmp1[:], ALU.mult).then_inc(u_ready, 1)

            def silu_z(m, par):
                dve.wait_ge(z_step, m * 3 + 3)
                dve.tensor_tensor(zs[:, par, :], tmp2[:, 0, :], tmp2[:, 1, :], ALU.mult).then_inc(zs_ready, 1)

            def gate(m, par):
                dve.wait_ge(hc_used, m * SUMS + SUMS)
                dve.wait_ge(zs_ready, m + 1)
                dve.tensor_tensor(yg[:, :], py[:, :], zs[:, par, :], ALU.mult).then_inc(gate_done, 1)

            def correction(m):
                dve.wait_ge(sp_step, m * 3 + 3)
                dve.scalar_tensor_tensor(tmp2[:], tmp2[:], -1.0, tmp0[:], ALU.add, ALU.subtract).then_inc(corr_done, 1)

            def log1p(m):
                dve.wait_ge(corr_done, m + 1)
                dve.tensor_tensor(tmp1[:], tmp1[:], tmp2[:], ALU.subtract).then_inc(log_done, 1)

            def make_delta(m):
                dve.wait_ge(log_done, m + 1)
                dve.tensor_tensor(delta[:], delta[:], tmp1[:], ALU.add).then_inc(delta_made, 1)

            def make_du(m):
                dve.wait_ge(delta_made, m + 1)
                dve.tensor_tensor(tmp1[:], delta[:], u[:], ALU.mult).then_inc(du_made, 1)

            def delta_rest(m):
                dve.wait_ge(split_step, m * 4 + 1)
                dve.tensor_tensor(tmp2[:], delta[:], parts[:, 0, 0, :].rearrange("p (d t) -> p d t", d=2),
                                  ALU.subtract).then_inc(drest_done, 1)

            def delta_last(m):
                dve.wait_ge(split_step, m * 4 + 3)
                dve.tensor_tensor(parts[:, 2, 0, :].rearrange("p (d t) -> p d t", d=2), tmp2[:],
                                  parts[:, 1, 0, :].rearrange("p (d t) -> p d t", d=2),
                                  ALU.subtract).then_inc(dparts_ready, 1)

            def read_out(o, m, i, odd):
                dve.wait_ge(out_ready, m + 1)
                if o == 0:
                    dve.tensor_copy(xrec[C * odd:C * odd + C, bass.ds(i * TOK, TOK)],
                                    pre[C * odd:C * odd + C, :]).then_inc(xrec_done, 1)
                else:
                    at = i * 2 * SEQS + (SEQS if odd else 0)
                    v = xrec[:].rearrange("p (r w) -> p r w", w=W)[:, :, bass.ds(at, SEQS)]
                    dve.tensor_tensor(v, v, pre[:, 0:SEQS * HALF].rearrange("p (s r) -> p r s", s=SEQS),
                                      ALU.add).then_inc(xrec_done, 1)

            def start(b, o, n0):
                if o == 0:
                    dve.wait_ge(final_done, b * 16)
                    for h in range(2):
                        r = slice(C * h, C * h + C)
                        dve.memset(xp[r, 0:PAD * S + PAD - h], 0.0)
                        at = (PAD + 1) * S - h
                        dve.memset(xp[r, at:at + (H - 1) * S].rearrange("p (r w) -> p r w", w=S)[:, :, 0:PAD], 0.0)
                        ins = dve.memset(xp[r, (H + PAD) * S - h:XP], 0.0)
                    ins.then_inc(pads_ready, 1)
                else:
                    dve.wait_ge(z_ready, b * PER_IMAGE + TILES)
                    dve.memset(xp[C:P, (H + PAD - 1) * S:(H + PAD) * S], 0.0).then_inc(pads_ready, 1)
                if o == 0:
                    dve.wait_ge(stored, b * 128)
                else:
                    dve.wait_ge(xrec_done, n0)
                read_conv(o, n0, 0)
                read_conv(o, n0, 1)
                read_z(n0)
                silu_u(n0)
                silu_z(n0, 0)
                for step in (correction, log1p, make_delta, make_du, delta_rest, delta_last):
                    step(n0)

            def body(o, k, n, par, first, last):
                m, mpar = n + 1, 1 - par
                for s in range(UNITS):
                    mulb(n, par, s, first)
                    if not last:
                        if s == 0:
                            read_conv(o, m, 0)
                        if s == 2:
                            read_conv(o, m, 1)
                        if s == 4:
                            read_z(m)
                        if s == 5:
                            silu_u(m)
                        if s == 8:
                            silu_z(m, mpar)
                        if s == 10:
                            correction(m)
                        if s == 11:
                            make_delta(m)
                        if s == 12:
                            delta_rest(m)
                    if not first:
                        if s == 3:
                            gate(n - 1, mpar)
                        if s == 6:
                            read_out(o, n - 1, k if par else k - 1, mpar)
                    scan(n, s)
                    if not last:
                        if s == 10:
                            log1p(m)
                        if s == 11:
                            make_du(m)
                        if s == 13:
                            delta_last(m)

            def flush(b, o, n):
                gate(n, 1)
                read_out(o, n, TILES // 2 - 1, 1)

            for b in phases(dve, start, body, flush):
                dve.wait_ge(xrec_done, b * PER_IMAGE + PER_IMAGE)
                for c in range(PIX // 512):
                    ins = dve.bn_stats(stats[:, c, :], xrec[:, c * 512:(c + 1) * 512])
                ins.then_inc(stat_done, 1)
                dve.wait_ge(stat_done, b * 10 + 1)
                dve.memset(st[:, 12:13], 0.0)
                dve.bn_aggr(st[:, 2:4], stats[:]).then_inc(stat_done, 1)
                dve.wait_ge(stat_done, b * 10 + 2)
                dve.tensor_copy(st[:, 0:1], st[:, 2:3])
                dve.scalar_tensor_tensor(st[:, 1:2], st[:, 2:3], st[:, 2:3], st[:, 3:4], ALU.mult,
                                         ALU.add).then_inc(stat_done, 1)
                dve.wait_ge(gm_ready, b + 1)
                dve.tensor_copy(st[:, 2:4], pre[:, 0:2]).then_inc(stat_done, 1)
                dve.wait_ge(stat_done, b * 10 + 4)
                dve.tensor_tensor(st[:, 4:5], st[:, 2:3], st[:, 2:3], ALU.mult).then_inc(stat_done, 1)
                dve.wait_ge(stat_done, b * 10 + 5)
                dve.tensor_tensor(st[:, 11:12], st[:, 3:4], st[:, 4:5], ALU.subtract).then_inc(stat_done, 1)
                dve.wait_ge(stat_done, b * 10 + 6)
                dve.tensor_scalar(st[:, 5:6], st[:, 11:12], 0.0, GN_EPS, ALU.max, ALU.add).then_inc(stat_done, 1)
                dve.wait_ge(rstd_step, b * 2 + 2)
                dve.tensor_tensor(st[:, 8:9], st[:, 7:8], gn_s[:, 0:1], ALU.mult).then_inc(stat_done, 1)
                dve.wait_ge(stat_done, b * 10 + 8)
                dve.tensor_tensor(st[:, 9:10], st[:, 2:3], st[:, 8:9], ALU.mult).then_inc(stat_done, 1)
                dve.wait_ge(stat_done, b * 10 + 9)
                dve.tensor_tensor(st[:, 10:11], gn_s[:, 1:2], st[:, 9:10], ALU.subtract).then_inc(stat_done, 1)
                for c in range(8):
                    dve.wait_ge(norm_done, b * 8 + c + 1)
                    dve.tensor_scalar(chunk(xrec, c), chunk(xrec, c), SILU_FLOOR, None, ALU.max).then_inc(floor_done, 1)
                dve.wait_ge(g_loaded, b * 32 + 32)
                for c in range(8):
                    dve.wait_ge(act_done, b * 8 + c + 1)
                    dve.tensor_tensor(g_chunk(c), g_chunk(c), chunk(xrec, c).rearrange("p (r w) -> p r w", w=W),
                                      ALU.add).then_inc(g_done, 1)
                dve.wait_ge(g_done, b * 8 + 8)
                e0 = 1 + b * 4
                dve.tensor_tensor(g_all[0:C, 0, 1:1 + W], g_all[0:C, 1, 1:1 + W], g_all[0:C, 2, 1:1 + W], ALU.add)
                dve.tensor_tensor(g_all[C:P, GR - 1, 1:1 + W], g_all[C:P, GR - 2, 1:1 + W],
                                  g_all[C:P, GR - 3, 1:1 + W], ALU.add).then_inc(edge_done, 1)
                dve.wait_ge(edge_done, e0 + 1)
                dve.tensor_scalar(g_all[0:C, 0, 1:1 + W], g_all[0:C, 0, 1:1 + W], 0.5, None, ALU.mult)
                dve.tensor_scalar(g_all[C:P, GR - 1, 1:1 + W], g_all[C:P, GR - 1, 1:1 + W], 0.5, None,
                                  ALU.mult).then_inc(edge_done, 1)
                dve.wait_ge(edge_done, e0 + 2)
                dve.wait_ge(halo_loaded, b * 32 + 32)
                dve.tensor_tensor(g_all[:, :, 0], g_all[:, :, 1], g_all[:, :, 2], ALU.add)
                dve.tensor_tensor(g_all[:, :, GW - 1], g_all[:, :, GW - 2], g_all[:, :, GW - 3],
                                  ALU.add).then_inc(edge_done, 1)
                dve.wait_ge(edge_done, e0 + 3)
                dve.tensor_scalar(g_all[:, :, 0], g_all[:, :, 0], 0.5, None, ALU.mult)
                dve.tensor_scalar(g_all[:, :, GW - 1], g_all[:, :, GW - 1], 0.5, None, ALU.mult).then_inc(edge_done, 1)
                dve.wait_ge(edge_done, e0 + 4)
                for c in range(4):
                    r0, r1 = (0 if c == 0 else 16 * c + 2), 16 * c + 18
                    dve.tensor_tensor(rows_all[:, r0:r1, :], g_all[:, r0:r1, 0:W], g_all[:, r0:r1, 1:1 + W],
                                      ALU.add).then_inc(rows_step, 1)
                    dve.wait_ge(rows_step, b * 4 + c + 1)
                    dve.tensor_tensor(rows_all[:, r0:r1, :], rows_all[:, r0:r1, :], g_all[:, r0:r1, 2:2 + W],
                                      ALU.add).then_inc(rows_done, 1)
                for c in range(PIX // 512):
                    dve.wait_ge(mix_ready, b * 16 + c + 1)
                    dve.scalar_tensor_tensor(
                        xrec[:, c * 512:(c + 1) * 512].rearrange("p (r w) -> p r w", w=W),
                        pd[:, (c // 2) % 2, c % 2, :].rearrange("p (r w) -> p r w", w=W), gn_s[:, 2:3],
                        g_all[:, 1 + SEQS * c:1 + SEQS * c + SEQS, 1:1 + W], ALU.add, ALU.add).then_inc(final_done, 1)

        @block.gpsimd
        def _(pool):
            def mulc(n, par, unit, first):
                d = unit_parts(unit)[0]
                if unit == 0:
                    pool.wait_ge(bc_read, n * 4 + 4)
                pool.wait_ge(scan_done, n * UNITS + unit + 1)
                if not (first and unit < 4):
                    pool.wait_ge(hc_used, n * SUMS + (unit - 4) // 2 + 1)
                pool.tensor_tensor(hc[:, unit % 4], hid[:, unit % 2, :, :],
                                   Cb[:, par, d, :].unsqueeze(1).to_broadcast([P, 2, TOK]), ALU.mult).then_inc(mulc_done, 1)

            def du_rest(m):
                pool.wait_ge(split_step, m * 4 + 2)
                pool.tensor_tensor(tmp0[:], tmp1[:], parts[:, 0, 1, :].rearrange("p (d t) -> p d t", d=2),
                                   ALU.subtract).then_inc(urest_done, 1)

            def du_last(m):
                pool.wait_ge(split_step, m * 4 + 4)
                pool.tensor_tensor(parts[:, 2, 1, :].rearrange("p (d t) -> p d t", d=2), tmp0[:],
                                   parts[:, 1, 1, :].rearrange("p (d t) -> p d t", d=2),
                                   ALU.subtract).then_inc(uparts_ready, 1)

            def start(b, o, n0):
                du_rest(n0)
                du_last(n0)

            def body(o, k, n, par, first, last):
                for s in range(UNITS):
                    mulc(n, par, s, first)
                    if not last:
                        if s == 11:
                            du_rest(n + 1)
                        if s == 12:
                            du_last(n + 1)

            for b in phases(pool, start, body, lambda b, o, n: None):
                for c in range(8):
                    pool.wait_ge(gate_step, b * 24 + 3 * c + 3)
                    pool.tensor_tensor(chunk(xrec, c), chunk(xrec, c), chunk(sig_all, c), ALU.mult).then_inc(act_done, 1)


def kernel(**inputs):
    import numpy as np
    import concourse.bacc as bacc
    from concourse.bass_utils import run_bass_kernel_spmd

    a = {k: np.asarray(v) for k, v in inputs.items()}

    def both(name, lay):
        return np.stack([lay(a[f"L0_conv_{o}_{name}"]) for o in ("row", "col")])

    di = a["L0_conv_row_D"].shape[0]
    c = a["x"].shape[1]
    p = np.arange(P)
    rows, m = np.arange(3 * 32), np.arange(P)
    sel = np.zeros((3 * 32, 4, P), np.float32)
    for q in range(4):
        sel[:, q, :] = (rows % 32)[:, None] == (8 * q + m // STATES)[None, :]
    statesum = np.zeros((P, 4, 32), np.float32)
    for j in range(4):
        statesum[:, j, :] = (8 * j + p // STATES)[:, None] == np.arange(32)[None, :]
    place = np.arange(di).reshape(4, 4, 8).transpose(1, 0, 2).reshape(-1)
    size = c // GN_GROUPS
    groupmean = ((p[:, None] % c) // size == (p[None, :] % c) // size).astype(np.float32) / (2 * size)
    ins = {
        "x": a["x"],
        "inT": both("in_w", lambda w: np.concatenate([w[:di], w[di:][place]]).T),
        "convT": both("conv_w", lambda w: w.reshape(di, TAPS).T.reshape(-1)),
        "xpT": both("xp_w", lambda w: w.T),
        "xpdt": both("xp_w", lambda w: w[:w.shape[0] - 2 * STATES]),
        "dtT": both("dt_w", lambda w: w.T),
        "alog": both("A_log", lambda w: w.reshape(-1, P).T),
        "chan": np.stack([both("conv_b", lambda w: w), both("dt_b", lambda w: w), both("D", lambda w: w)], -1),
        "outT": both("out_w", lambda w: w.T[place]),
        "gn": np.stack([a["L0_conv_gn_w"], a["L0_conv_gn_b"], a["L1_conv_conv_b"]], -1),
        "mixT": a["L1_conv_conv_w"].T,
        "eye": np.eye(P, dtype=np.float32)[place],
        "sel": sel.reshape(3 * 32, -1),
        "statesum": statesum.reshape(P, -1),
        "groupmean": groupmean,
    }
    nc = bacc.Bacc("TRN2", target_bir_lowering=False, num_devices=1)
    arrays, args = {}, []
    for name, v in ins.items():
        v = np.ascontiguousarray(v)
        arrays[f"in_{name}_dram"] = v
        args.append(nc.dram_tensor(f"in_{name}_dram", v.shape, mybir.dt.from_np(v.dtype), kind="ExternalInput").ap())
    args.append(nc.dram_tensor("out_dram", a["x"].shape, F32, kind="ExternalOutput").ap())
    build(nc, *args)
    r = run_bass_kernel_spmd(nc, [arrays], core_ids=[0])
    return r.results[0]["out_dram"]
```

```python
from contextlib import ExitStack

import concourse.bass as bass
from concourse import mybir

ALU = mybir.AluOpType
ACT = mybir.ActivationFunctionType
F32 = mybir.dt.float32
BF16 = mybir.dt.bfloat16

P = 128
TAPS = 4
STATES = 16
SEQS = 4
UNITS = 16
LAG = 6
SILU_FLOOR = -44.0
GN_GROUPS = 4
GN_EPS = 1e-5


def unit_parts(unit):
    return unit // 8, (unit // 2) % 4, (2 * (unit % 2), 2 * (unit % 2) + 1)


def build(nc, x, inT, convT, xpT, xpdt, dtT, alog, chan, outT, gn, mixT, eye, sel, statesum, groupmean, out):
    B, C, H, W = x.shape
    DI = 2 * C
    L = W
    TOK = SEQS * L
    TILES = H // SEQS
    PER_IMAGE = 2 * TILES
    HALF = H // 2
    PIX = HALF * W
    XPW = xpT.shape[-1]
    S = W + TAPS - 1
    PAD = TAPS - 1
    XP = (H + 2 * PAD) * S + PAD
    GW = W + 2
    GR = HALF + 2
    HS_AT = GR * GW
    assert H == W == P and DI == P and HS_AT + GR * W <= XP and PER_IMAGE == 64

    with ExitStack() as ctx:
        def sb(name, shape, dt=F32):
            return ctx.enter_context(nc.sbuf_tensor(name, shape, dt))

        def sem(name):
            return ctx.enter_context(nc.semaphore(name))

        xp = sb("xp", [P, XP])
        xrec = sb("xrec", [P, PIX])
        u = sb("u", [P, 2, 2, TOK])
        delta = sb("delta", [P, 2, TOK])
        parts = sb("parts", [P, 3, 2, 2 * TOK], BF16)
        ring = sb("ring", [3 * 32, 4, 2, TOK], BF16)
        Bb = sb("Bb", [P, 2, TOK])
        Cb = sb("Cb", [P, 2, TOK])
        tmp0 = sb("tmp0", [P, 2, TOK])
        tmp1 = sb("tmp1", [P, 2, TOK])
        tmp2 = sb("tmp2", [P, 2, TOK])
        decay = sb("decay", [P, 2, 2, SEQS, L])
        hid = sb("hid", [P, 4, 2, TOK])
        hc = sb("hc", [P, 4, 2, TOK])
        zs = sb("zs", [P, TOK])
        conv_w = sb("conv_w", [P, 2, 4, P])
        z_w = sb("z_w", [P, 2, P])
        dt_w = sb("dt_w", [P, 2, P])
        B_w = sb("B_w", [P, 2, P])
        C_w = sb("C_w", [P, 2, P])
        D_w = sb("D_w", [P, 2, P])
        out_w = sb("out_w", [P, 2, C])
        A_s = sb("A_s", [P, 2, STATES])
        chan_s = sb("chan_s", [P, 2, 3])
        gn_s = sb("gn_s", [P, 3])
        sel_s = sb("sel_s", [3 * 32, 4, P], BF16)
        sum_s = sb("sum_s", [P, 4, 32])
        mean_s = sb("mean_s", [P, P])
        mix_s = sb("mix_s", [P, P])
        stats = sb("stats", [P, PIX // 512, 6])
        st = sb("st", [P, 16])

        pd = ctx.enter_context(nc.psum_tensor("pd", [P, 2, 512], F32))
        pu = ctx.enter_context(nc.psum_tensor("pu", [P, 2, 2, 512], F32))
        py = ctx.enter_context(nc.psum_tensor("py", [P, 512], F32))
        pre = ctx.enter_context(nc.psum_tensor("pre", [P, 512], F32))

        loaded = sem("weights_loaded")
        w_dve = sem("weights_made")
        w_exp = sem("a_exp_done")
        w_pe = sem("dt_product_ready")
        x_first = sem("x_first_rows_loaded")
        x_loaded = sem("x_loaded")
        x_shifted = sem("x_shifted")
        pads_ready = sem("pads_ready")
        delta_ready = sem("delta_ready")
        du_ready = sem("du_ready")
        hc_used = sem("hc_used")
        conv_ready = sem("conv_ready")
        z_ready = sem("z_ready")
        dpre_ready = sem("dpre_ready")
        bc_ready = sem("bc_ready")
        out_ready = sem("out_ready")
        ring_loaded = [sem(f"ring_loaded_{j}") for j in range(4)]
        exp_done = sem("exp_done")
        silu_step = sem("silu_step")
        z_step = sem("z_step")
        dpre_read = sem("dpre_read")
        sp_step = sem("sp_step")
        split_step = sem("split_step")
        bc_read = sem("bc_read")
        mulb_done = sem("mulb_done")
        scan_done = sem("scan_done")
        conv_read = sem("conv_read")
        z_read = sem("z_read")
        gate_done = sem("gate_done")
        corr_done = sem("corr_done")
        log_done = sem("log_done")
        delta_made = sem("delta_made")
        du_made = sem("du_made")
        dparts_ready = sem("dparts_ready")
        xrec_done = sem("xrec_done")
        mulc_done = sem("mulc_done")
        u_ready = sem("u_ready")
        zs_ready = sem("zs_ready")
        drest_done = sem("drest_done")
        urest_done = sem("urest_done")
        uparts_ready = sem("uparts_ready")
        g_loaded = sem("g_loaded")
        stat_done = sem("stat_done")
        gm_ready = sem("gm_ready")
        rstd_step = sem("rstd_step")
        norm_done = sem("norm_done")
        floor_done = sem("floor_done")
        gate_step = sem("gate_step")
        act_done = sem("act_done")
        g_done = sem("g_done")
        halo_loaded = sem("halo_loaded")
        edge_done = sem("edge_done")
        rows_step = sem("rows_step")
        rows_done = sem("rows_done")
        mix_ready = sem("mix_ready")
        final_done = sem("final_done")
        stored = sem("stored")

        ST = 1088

        def scratch(o, at, n):
            return xrec[:, o * ST + at:o * ST + at + n]
        in_t = [scratch(o, 0, 256) for o in range(2)]
        cw_t = [scratch(o, 256, 512) for o in range(2)]
        xp_t = [scratch(o, 768, XPW) for o in range(2)]
        al_t = [scratch(o, 804, 16) for o in range(2)]
        xd_t = [scratch(o, 820, P) for o in range(2)]
        dt_t = [scratch(o, 948, P) for o in range(2)]
        eye_t = xrec[:, 2 * ST:2 * ST + P]
        mix_t = xrec[:, 2 * ST + P:2 * ST + 2 * P]
        sel_t = xrec[0:3 * 32, 2 * ST + 2 * P:2 * ST + 6 * P]

        def window(o, i, odd, shift):
            if o == 0:
                at = (i * SEQS + (HALF if odd else 0) + PAD) * S + PAD + shift
                return xp[:, bass.ds(at, SEQS * S)].rearrange("p (s w) -> p s w", w=S)[:, :, 0:L]
            at = i * 2 * SEQS + (SEQS if odd else 0) + PAD + (PAD + shift) * S
            return xp[:, bass.ds(at, L * S)].rearrange("p (t w) -> p w t", w=S)[:, 0:SEQS, :]

        def tokens(ap, backward):
            a = ap.rearrange("p (s t) -> p s t", s=SEQS)
            return a[:, :, L - 1::-1] if backward else a

        g_all = xp[:, 0:GR * GW].rearrange("p (r w) -> p r w", w=GW)
        rows_all = xp[:, HS_AT:HS_AT + GR * W].rearrange("p (r w) -> p r w", w=W)
        CH = PIX // 8
        CR = CH // W
        ENDS_FIRST = (0, 7, 1, 2, 3, 4, 5, 6)

        def chunk(ap, c):
            return ap[:, c * CH:(c + 1) * CH]

        def start_bank(odd, direction):
            return pu[:, odd, direction, :]

        def silu_scratch(second):
            return (hc[:, 2], hc[:, 3]) if second else (tmp0, tmp1)

        def gate_buffer(k):
            return (tmp0, tmp1, tmp2)[k % 3][:].rearrange("p d t -> p (d t)")

        def g_chunk(c):
            return g_all[:, 1 + c * CR:1 + (c + 1) * CR, 1:1 + W]

        def phases(eng, start, body, flush):
            with eng.Fori(0, B) as b:
                for o in range(2):
                    n0 = b * PER_IMAGE + o * TILES
                    start(b, o, n0)
                    body(o, 0, n0, 0, True, True, True)
                    with eng.Fori(0, TILES // 2 - 2) as k:
                        body(o, k, n0 + 2 * k + 1, 1, False, True, True)
                        body(o, k + 1, n0 + 2 * k + 2, 0, False, True, True)
                    body(o, TILES // 2 - 2, n0 + TILES - 3, 1, False, True, True)
                    body(o, TILES // 2 - 1, n0 + TILES - 2, 0, False, False, True)
                    body(o, TILES // 2 - 1, n0 + TILES - 1, 1, False, False, False)
                    flush(b, o, n0 + TILES - 1)
                    if o == 1:
                        yield b

        block = ctx.enter_context(nc.Block())

        @block.sync
        def _(sp):
            for o in range(2):
                for h in range(2):
                    sp.dma_start(in_t[o][C * h:C * h + C, :], inT[o]).then_inc(loaded, 16)
                sp.dma_start(cw_t[o], convT[o].partition_broadcast(P)).then_inc(loaded, 16)
                sp.dma_start(xp_t[o], xpT[o]).then_inc(loaded, 16)
                sp.dma_start(al_t[o], alog[o]).then_inc(loaded, 16)
                sp.dma_start(xd_t[o][0:4, :], xpdt[o]).then_inc(loaded, 16)
                sp.dma_start(dt_t[o][0:4, :], dtT[o]).then_inc(loaded, 16)
                sp.dma_start(chan_s[:, o, :], chan[o]).then_inc(loaded, 16)
                sp.dma_start(out_w[:, o, :], outT[o]).then_inc(loaded, 16)
            for h in range(2):
                sp.dma_start(gn_s[C * h:C * h + C, :], gn).then_inc(loaded, 16)
                sp.dma_start(mix_t[C * h:C * h + C, 0:C], mixT).then_inc(loaded, 16)
            sp.dma_start(eye_t, eye).then_inc(loaded, 16)
            sp.dma_start(sel_t, sel).then_inc(loaded, 16)
            sp.dma_start(sum_s[:].rearrange("p j m -> p (j m)"), statesum).then_inc(loaded, 16)
            sp.dma_start(mean_s[:], groupmean).then_inc(loaded, 16)

            def interior(lo, shift):
                at = PAD * S + PAD - shift
                a = xp[lo:lo + C, at:at + H * S].rearrange("p (r w) -> p r w", w=S)
                return a[:, :, 0:W]

            def load_ring(n, first):
                for step in range(8):
                    d, j = step // 4, step % 4
                    if step == 0:
                        sp.wait_ge(uparts_ready, n + 1)
                    elif step >= (4 if first else 1):
                        sp.wait_ge(delta_ready, (n * UNITS + 2 * step - 6) * 2)
                    for k in range(3):
                        sp.dma_start(ring[32 * k:32 * k + 32, j, :, :],
                                     parts[32 * j:32 * j + 32, k, :, d * TOK:(d + 1) * TOK]).then_inc(ring_loaded[j], 16)

            def tiles(n0):
                load_ring(n0, True)
                with sp.Fori(1, TILES) as i:
                    load_ring(n0 + i, False)

            with sp.Fori(0, B) as b:
                image = x[bass.ds(b, 1)].rearrange("a c h w -> (a c) h w")
                pads = sp.snap(b * 2 + 1)
                sp.wait_ge(final_done, b * 16)
                sp.wait_ge(pads_ready, pads)
                for ready, lo, hi in ((x_first, 0, 16), (x_loaded, 16, HALF)):
                    for top in (0, HALF):
                        rows = slice(top + lo, top + hi)
                        for upper in range(2):
                            sp.dma_start(interior(C * upper, upper)[:, rows, :], image[:, rows, :]).then_inc(ready, 16)
                tiles(b * PER_IMAGE)
                sp.wait_ge(z_ready, b * PER_IMAGE + TILES)
                sp.dma_start(interior(C, S), image).then_inc(x_shifted, 16)
                tiles(b * PER_IMAGE + TILES)
                sp.wait_ge(z_ready, b * PER_IMAGE + PER_IMAGE)
                for h in range(2):
                    sp.dma_start(g_all[C * h:C * h + C, 1:1 + HALF, 1:1 + W],
                                 image[:, HALF * h:HALF * h + HALF, :]).then_inc(g_loaded, 16)
                sp.wait_ge(g_done, b * 8 + 2)
                sp.dma_start(g_all[0:C, GR - 1, 1:1 + W], g_all[C:P, 1, 1:1 + W]).then_inc(halo_loaded, 16)
                sp.dma_start(g_all[C:P, 0, 1:1 + W], g_all[0:C, GR - 2, 1:1 + W]).then_inc(halo_loaded, 16)
                result = out[bass.ds(b, 1)].rearrange("a c h w -> (a c) (h w)")
                for c in range(4):
                    sp.wait_ge(final_done, b * 16 + 4 * c + 4)
                    for h in range(2):
                        sp.dma_start(result[:, h * PIX + c * (PIX // 4):h * PIX + (c + 1) * (PIX // 4)],
                                     xrec[C * h:C * h + C, c * (PIX // 4):(c + 1) * (PIX // 4)]
                                     ).then_inc(stored, 16)
            sp.wait_ge(stored, B * 128)

        N_LOADS = 2 * 9 + 4 + 4

        @block.tensor
        def _(pe):
            pe.wait_ge(loaded, 16 * N_LOADS)
            for o in range(2):
                if o == 1:
                    pe.wait_ge(w_dve, 1)
                pe.matmul(pre[:, 0:P], xd_t[o][0:4, :], dt_t[o][0:4, :], start=True, stop=True).then_inc(w_pe, 1)
            pe.wait_ge(w_dve, 3)

            def conv(o, i, odd, direction, bank=pre):
                w = conv_w[:, o, 2 * direction:2 * direction + 2, :]
                first, second = ((-3, -1), (0, 2))[direction]
                pe.matmul(bank[:, :], w[:, 0, :], window(o, i, odd, first), start=True, stop=False)
                pe.matmul(bank[:, :], w[:, 1, :], window(o, i, odd, second),
                          start=False, stop=True).then_inc(conv_ready, 1)

            def fill_z(o, i, odd):
                pe.matmul(pre[:, :], z_w[:, o, :], window(o, i, odd, 0), start=True, stop=True).then_inc(z_ready, 1)

            def fill_dpre(o, m, par, direction, bank=pre):
                if direction == 0:
                    pe.wait_ge(u_ready, m + 1)
                elif bank is pre:
                    pe.wait_ge(dpre_read, m * 2 + 1)
                pe.matmul(bank[:, :], dt_w[:, o, :], u[:, par, direction, :],
                          start=True, stop=True).then_inc(dpre_ready, 1)

            def fill_bc(o, par, k):
                pe.matmul(pre[:, :], (B_w, C_w)[k % 2][:, o, :], u[:, par, k // 2, :],
                          start=True, stop=True).then_inc(bc_ready, 1)

            def spread(n, unit, tensor, bank, q):
                d, j, _ = unit_parts(unit)
                if tensor == 1 and q == 0:
                    pe.wait_ge(ring_loaded[j], n * 96 + 48 * d + 48)
                return pe.matmul(bank, sel_s[:, q, :], ring[:, j, tensor, :], start=True, stop=True)

            def spread_du(n, unit, first):
                if not (first and unit < 2):
                    pe.wait_ge(mulb_done, n * UNITS + unit - 1)
                for k, q in enumerate(unit_parts(unit)[2]):
                    mm = spread(n, unit, 1, pu[:, unit % 2, k, :], q)
                mm.then_inc(du_ready, 1)

            def spread_delta(n, unit, first):
                for k, q in enumerate(unit_parts(unit)[2]):
                    if not (first and unit == 0):
                        pe.wait_ge(exp_done, (n * UNITS + unit) * 2 - 1 + k)
                    spread(n, unit, 0, pd[:, k, :], q).then_inc(delta_ready, 1)

            def state_sum(n, pair):
                d, j, _ = unit_parts(2 * pair)
                pe.wait_ge(mulc_done, n * UNITS + 2 * pair + 2)
                for q in range(4):
                    mm = pe.matmul(py[32 * q:32 * q + 32, :], sum_s[:, j, :],
                                   tokens(hc[:, (2 * pair + q // 2) % 4, q % 2, :], d),
                                   start=False, stop=(pair == UNITS // 2 - 1), skip_group_check=True)
                mm.then_inc(hc_used, 1)

            def skip_term(o, n, par, first):
                if not first:
                    pe.wait_ge(gate_done, n)
                pe.matmul(py[:, :], D_w[:, o, :], u[:, par, 0, :], start=True, stop=False, skip_group_check=True)
                pe.matmul(py[:, :], D_w[:, o, :], tokens(u[:, par, 1, :], 1), start=False, stop=False,
                          skip_group_check=True)

            def fill_out(o, m, odd):
                pe.wait_ge(gate_done, m + 1)
                if o == 0:
                    pe.matmul(pre[C * odd:C * odd + C, :], out_w[:, o, :], zs[:, :],
                              start=True, stop=True).then_inc(out_ready, 1)
                else:
                    v = zs[:, :].rearrange("p (s t) -> p s t", s=SEQS)
                    for h in range(2):
                        mm = pe.matmul(pre[C * h:C * h + C, 0:SEQS * HALF], out_w[:, o, :],
                                       v[:, :, HALF * h:HALF * h + HALF], start=True, stop=True)
                    mm.then_inc(out_ready, 1)

            def start(b, o, n0):
                if o == 0:
                    pe.wait_ge(x_first, b * 64 + 64)
                else:
                    pe.wait_ge(x_shifted, b * 16 + 16)
                pe.wait_ge(pads_ready, b * 2 + o + 1)
                pe.wait_ge(xrec_done, n0)
                for odd in range(2):
                    for d in range(2):
                        conv(o, 0, odd, d, start_bank(odd, d))
                for d in range(2):
                    fill_dpre(o, n0, 0, d, pd[:, d, :])
                for k in range(2):
                    if k:
                        pe.wait_ge(bc_read, n0 * 4 + 1)
                    fill_bc(o, 0, k)
                pe.wait_ge(conv_read, n0 * 2 + 4)
                pe.wait_ge(dpre_read, n0 * 2 + 2)

            def body(o, i, n, par, first, stage_a, stage_b):
                m, mpar = n + 1, 1 - par
                for s in range(UNITS):
                    spread_du(n, s, first)
                    spread_delta(n, s, first)
                    if s == LAG:
                        skip_term(o, n, par, first)
                    if s % 2 == 0 and s >= LAG:
                        state_sum(n, (s - LAG) // 2)
                    elif s % 2 == 0 and not first:
                        state_sum(n - 1, (UNITS + s - LAG) // 2)
                    if s == 1:
                        pe.wait_ge(bc_read, n * 4 + 2)
                        fill_bc(o, par, 2)
                    if stage_b and s == 3:
                        pe.wait_ge(bc_read, n * 4 + 3)
                        fill_dpre(o, m, mpar, 0)
                    if stage_b and s == 4:
                        fill_dpre(o, m, mpar, 1)
                    if s == 5:
                        if stage_b:
                            pe.wait_ge(dpre_read, m * 2 + 2)
                        else:
                            pe.wait_ge(bc_read, n * 4 + 3)
                        fill_bc(o, par, 3)
                    if not first and s == 7:
                        pe.wait_ge(bc_read, n * 4 + 4)
                        fill_out(o, n - 1, mpar)
                    if stage_b and s == 8:
                        if first:
                            pe.wait_ge(bc_read, n * 4 + 4)
                        else:
                            pe.wait_ge(xrec_done, n)
                        fill_bc(o, mpar, 0)
                    if stage_a and s == 12:
                        pe.wait_ge(bc_read, m * 4 + 1)
                        if first and o == 0:
                            pe.wait_ge(x_loaded, n + 64)
                        conv(o, i + 1, par, 0)
                    if stage_a and s == 13:
                        pe.wait_ge(conv_read, (m + 1) * 2 + 1)
                        conv(o, i + 1, par, 1)
                    if s == 14:
                        if stage_a:
                            pe.wait_ge(conv_read, (m + 1) * 2 + 2)
                        elif stage_b:
                            pe.wait_ge(bc_read, m * 4 + 1)
                        else:
                            pe.wait_ge(xrec_done, n)
                        fill_z(o, i, par)
                    if stage_b and s == 15:
                        pe.wait_ge(z_read, n + 1)
                        fill_bc(o, mpar, 1)

            def flush(b, o, n):
                for pair in range((UNITS - LAG) // 2, UNITS // 2):
                    state_sum(n, pair)
                pe.wait_ge(z_read, n + 1)
                fill_out(o, n, 1)

            for b in phases(pe, start, body, flush):
                pe.wait_ge(stat_done, b * 10 + 3)
                pe.matmul(pre[:, 0:2], mean_s[:], st[:, 0:2], start=True, stop=True).then_inc(gm_ready, 1)
                for c in range(PIX // 512):
                    if c == 0 or (c % 2 == 1 and c < PIX // 512 - 1):
                        pe.wait_ge(rows_done, b * 8 + (c + 1) // 2 + 1)
                    if c >= 4:
                        pe.wait_ge(final_done, b * 16 + c - 3)
                    for r in range(3):
                        mm = pe.matmul(pu[:, (c // 2) % 2, c % 2, :], mix_s[:],
                                       rows_all[:, SEQS * c + r:SEQS * c + r + SEQS, :],
                                       start=(r == 0), stop=(r == 2))
                    mm.then_inc(mix_ready, 1)

        @block.scalar
        def _(act):
            act.preload_act_table_set("natural_log_exp_and_others")
            act.wait_ge(loaded, 16 * N_LOADS)
            for o in range(2):
                act.activation(A_s[:, o, :], al_t[o], ACT.Exp).then_inc(w_exp, 1)
            act.wait_ge(w_dve, 3)

            def exps(o, n, unit, first):
                _, j, quads = unit_parts(unit)
                if not (first and unit < 2):
                    act.wait_ge(scan_done, n * UNITS + unit - 1)
                for k, q in enumerate(quads):
                    act.wait_ge(delta_ready, (n * UNITS + unit) * 2 + k + 1)
                    v = pd[:, k, :].rearrange("p (s t) -> p s t", s=SEQS)
                    act.activation(decay[:, unit % 2, k, :, 1:L], v[:, :, 1:L], ACT.Exp,
                                   scale=A_s[:, o, 4 * j + q:4 * j + q + 1]).then_inc(exp_done, 1)

            def silu_sigmoid(m, step, second=False):
                t0, t1 = (t[:, :, :].rearrange("p d t -> p (d t)") for t in silu_scratch(second))
                if step == 0:
                    act.wait_ge(conv_read, m * 2 + 2)
                    act.activation(t1, t0, ACT.Exp, scale=-1.0).then_inc(silu_step, 1)
                elif step == 1:
                    act.wait_ge(silu_step, m * 3 + 1)
                    act.activation(t1, t1, ACT.Ln, bias=1.0).then_inc(silu_step, 1)
                else:
                    act.wait_ge(silu_step, m * 3 + 2)
                    act.activation(t1, t1, ACT.Exp, scale=-1.0).then_inc(silu_step, 1)

            def z_sigmoid(m, step):
                zin, zout = tmp2[:, 0, :], tmp2[:, 1, :]
                if step == 0:
                    act.wait_ge(z_read, m + 1)
                    act.activation(zout, zin, ACT.Exp, scale=-1.0).then_inc(z_step, 1)
                elif step == 1:
                    act.wait_ge(z_step, m * 3 + 1)
                    act.activation(zout, zout, ACT.Ln, bias=1.0).then_inc(z_step, 1)
                else:
                    act.wait_ge(z_step, m * 3 + 2)
                    act.activation(zout, zout, ACT.Exp, scale=-1.0).then_inc(z_step, 1)

            def read_dpre(o, m, d, bank=pre):
                act.wait_ge(dpre_ready, m * 2 + d + 1)
                act.activation(tmp0[:, d, :], bank[:, :], ACT.Abs, bias=chan_s[:, o, 1:2])
                act.activation(delta[:, d, :], bank[:, :], ACT.Relu, bias=chan_s[:, o, 1:2]).then_inc(dpre_read, 1)

            def softplus(m, step, body):
                t0, t1, t2 = (t[:].rearrange("p d t -> p (d t)") for t in (tmp0, tmp1, tmp2))
                if step == 0:
                    act.wait_ge(dpre_read, m * 2 + 2)
                    act.activation(t0, t0, ACT.Exp, scale=-1.0).then_inc(sp_step, 1)
                elif step == 1:
                    act.wait_ge(sp_step, m * 3 + 1)
                    act.activation(t1, t0, ACT.Ln, bias=1.0).then_inc(sp_step, 1)
                else:
                    if body:
                        act.wait_ge(zs_ready, m - 1)
                    act.activation(t2, t0, ACT.Identity, bias=1.0).then_inc(sp_step, 1)

            def split(m, step):
                part, tensor = divmod(step, 2)
                if step == 0:
                    for j in range(4):
                        act.wait_ge(ring_loaded[j], m * 96)
                    act.wait_ge(delta_made, m + 1)
                elif step == 1:
                    act.wait_ge(du_made, m + 1)
                else:
                    act.wait_ge((drest_done, urest_done)[tensor], m + 1)
                whole = ((delta, tmp1), (tmp2, tmp0))[part][tensor]
                act.activation(parts[:, part, tensor, :], whole[:].rearrange("p d t -> p (d t)"),
                               ACT.Copy).then_inc(split_step, 1)

            def read_bc(m, k, used):
                act.wait_ge(bc_ready, m * 4 + k + 1)
                act.wait_ge((mulb_done, mulc_done)[k % 2], used)
                act.activation((Bb, Cb)[k % 2][:, k // 2, :], pre[:, :], ACT.Copy).then_inc(bc_read, 1)

            def start(b, o, n0):
                act.wait_ge(xrec_done, n0)
                for step in range(3):
                    silu_sigmoid(n0, step)
                silu_sigmoid(n0 + 1, 0, True)
                for d in range(2):
                    read_dpre(o, n0, d, pd[:, d, :])
                for step in range(3):
                    softplus(n0, step, False)
                silu_sigmoid(n0 + 1, 1, True)
                split(n0, 0)
                split(n0, 1)
                for k in range(2):
                    read_bc(n0, k, n0 * UNITS)
                split(n0, 2)
                split(n0, 3)
                silu_sigmoid(n0 + 1, 2, True)

            def body(o, i, n, par, first, stage_a, stage_b):
                m, mpar = n + 1, 1 - par
                for s in range(UNITS):
                    exps(o, n, s, first)
                    if s == 0:
                        read_bc(n, 2, n * UNITS)
                        if not first:
                            z_sigmoid(n - 1, 1)
                    if s == 1 and not first:
                        z_sigmoid(n - 1, 2)
                    if stage_b:
                        if s in (3, 4):
                            read_dpre(o, m, s - 3)
                        if s in (4, 5, 6):
                            softplus(m, s - 4, True)
                        if s in (7, 8):
                            split(m, s - 7)
                        if s == 8:
                            read_bc(m, 0, n * UNITS + 8)
                        if s == 9:
                            split(m, 2)
                            split(m, 3)
                    if s == 6:
                        read_bc(n, 3, n * UNITS)
                    if stage_a and s == 13:
                        silu_sigmoid(m + 1, 0)
                    if stage_a and s == 14:
                        silu_sigmoid(m + 1, 1)
                    if s == 15:
                        if stage_a:
                            silu_sigmoid(m + 1, 2)
                        if stage_b:
                            read_bc(m, 1, n * UNITS + 8)
                        z_sigmoid(n, 0)

            def flush(b, o, n):
                z_sigmoid(n, 1)
                z_sigmoid(n, 2)

            for b in phases(act, start, body, flush):
                act.wait_ge(stat_done, b * 10 + 7)
                act.activation(st[:, 6:7], st[:, 5:6], ACT.Ln).then_inc(rstd_step, 1)
                act.wait_ge(rstd_step, b * 2 + 1)
                act.activation(st[:, 7:8], st[:, 6:7], ACT.Exp, scale=-0.5).then_inc(rstd_step, 1)
                for k in range(8):
                    t = gate_buffer(k)
                    act.wait_ge(floor_done, b * 8 + k + 1)
                    if k >= 3:
                        act.wait_ge(act_done, b * 8 + k - 2)
                    act.activation(t, chunk(xrec, ENDS_FIRST[k]), ACT.Exp, scale=-1.0).then_inc(gate_step, 1)
                    act.wait_ge(gate_step, b * 24 + 3 * k + 1)
                    act.activation(t, t, ACT.Ln, bias=1.0).then_inc(gate_step, 1)
                    act.wait_ge(gate_step, b * 24 + 3 * k + 2)
                    act.activation(t, t, ACT.Exp, scale=-1.0).then_inc(gate_step, 1)

        @block.vector
        def _(dve):
            dve.memset(decay[:], 0.0)
            dve.memset(z_w[:], 0.0)
            dve.memset(mix_s[:], 0.0).then_inc(edge_done, 1)
            dve.wait_ge(edge_done, 1)
            dve.wait_ge(loaded, 16 * N_LOADS)
            for o in range(2):
                for m, (lower, upper) in enumerate(((0, 1), (2, 3), (3, 2), (1, 0))):
                    for h, tap in ((0, lower), (1, upper)):
                        r = slice(C * h, C * h + C)
                        dve.tensor_tensor(conv_w[r, o, m, :], in_t[o][r, 0:P], cw_t[o][r, tap * P:tap * P + P], ALU.mult)
                dve.tensor_copy(z_w[0:C, o, :], in_t[o][0:C, P:2 * P])
                for w, at in ((B_w, XPW - 2 * STATES), (C_w, XPW - STATES)):
                    dve.tensor_copy(w[:, o, :].rearrange("p (c n) -> p c n", n=STATES),
                                    xp_t[o][:, at:at + STATES].unsqueeze(1).to_broadcast([P, P // STATES, STATES]))
                dve.tensor_scalar(D_w[:, o, :], eye_t, chan_s[:, o, 2:3], None, ALU.mult)
                dve.tensor_scalar(out_w[:, o, :], out_w[:, o, :], 0.25, None, ALU.mult)
                dve.wait_ge(w_exp, o + 1)
                dve.tensor_scalar(A_s[:, o, :], A_s[:, o, :], -1.0, None, ALU.mult)
                dve.wait_ge(w_pe, o + 1)
                dve.tensor_copy(dt_w[:, o, :], pre[:, 0:P]).then_inc(w_dve, 1)
            dve.tensor_copy(sel_s[:].rearrange("p j m -> p (j m)"), sel_t)
            for h in range(2):
                r = slice(C * h, C * h + C)
                ins = dve.tensor_scalar(mix_s[r, C * h:C * h + C], mix_t[r, 0:C], 1.0 / 9.0, None, ALU.mult)
            ins.then_inc(w_dve, 1)
            dve.wait_ge(w_dve, 3)

            def mulb(n, unit, first):
                d = unit_parts(unit)[0]
                if unit % 8 == 0:
                    dve.wait_ge(bc_read, n * 4 + 2 * d + 1)
                dve.wait_ge(du_ready, n * UNITS + unit + 1)
                if not (first and unit < 4):
                    dve.wait_ge(mulc_done, n * UNITS + unit - 3)
                dve.tensor_tensor(hid[:, unit % 4, :, :], pu[:, unit % 2, :, :],
                                  Bb[:, d, :].unsqueeze(1).to_broadcast([P, 2, TOK]), ALU.mult).then_inc(mulb_done, 1)

            def scan(n, unit):
                dve.wait_ge(exp_done, (n * UNITS + unit) * 2 + 2)
                dve.wait_ge(mulb_done, n * UNITS + unit + 1)
                h = hid[:, unit % 4, :, :].rearrange("p g t -> p (g t)")
                dve.tensor_tensor_scan(h, decay[:, unit % 2].rearrange("p g s t -> p (g s t)"), h, 0.0,
                                       ALU.mult, ALU.add).then_inc(scan_done, 1)

            def read_conv(o, m, d, bank=pre, second=False):
                dve.wait_ge(conv_ready, m * 2 + d + 1)
                if not second:
                    dve.wait_ge(uparts_ready, m)
                dve.tensor_scalar(tokens(silu_scratch(second)[0][:, d, :], 0), tokens(bank[:, :], d),
                                  chan_s[:, o, 0:1], SILU_FLOOR, ALU.add, ALU.max).then_inc(conv_read, 1)

            def read_z(m, stage_b):
                dve.wait_ge(dparts_ready, m + 1 + stage_b)
                dve.wait_ge(z_ready, m + 1)
                dve.tensor_scalar(tmp2[:, 0, :], pre[:, :], SILU_FLOOR, None, ALU.max).then_inc(z_read, 1)

            def gate(m):
                dve.wait_ge(hc_used, (m + 1) * (UNITS // 2))
                dve.wait_ge(zs_ready, m + 1)
                dve.tensor_tensor(zs[:, :], py[:, :], zs[:, :], ALU.mult).then_inc(gate_done, 1)

            def correction(m):
                dve.wait_ge(sp_step, m * 3 + 3)
                dve.scalar_tensor_tensor(tmp2[:], tmp2[:], -1.0, tmp0[:], ALU.add, ALU.subtract).then_inc(corr_done, 1)

            def log1p(m):
                dve.wait_ge(corr_done, m + 1)
                dve.tensor_tensor(tmp1[:], tmp1[:], tmp2[:], ALU.subtract).then_inc(log_done, 1)

            def make_delta(m):
                dve.wait_ge(log_done, m + 1)
                dve.tensor_tensor(delta[:], delta[:], tmp1[:], ALU.add).then_inc(delta_made, 1)

            def make_du(m, par):
                dve.wait_ge(delta_made, m + 1)
                dve.tensor_tensor(tmp1[:], delta[:], u[:, par], ALU.mult).then_inc(du_made, 1)

            def delta_rest(m):
                dve.wait_ge(split_step, m * 4 + 1)
                dve.tensor_tensor(tmp2[:], delta[:], parts[:, 0, 0, :].rearrange("p (d t) -> p d t", d=2),
                                  ALU.subtract).then_inc(drest_done, 1)

            def delta_last(m):
                dve.wait_ge(split_step, m * 4 + 3)
                dve.tensor_tensor(parts[:, 2, 0, :].rearrange("p (d t) -> p d t", d=2), tmp2[:],
                                  parts[:, 1, 0, :].rearrange("p (d t) -> p d t", d=2),
                                  ALU.subtract).then_inc(dparts_ready, 1)

            def first_u(m):
                dve.wait_ge(silu_step, m * 3 + 3)
                dve.tensor_tensor(u[:, 0], tmp0[:], tmp1[:], ALU.mult).then_inc(u_ready, 1)

            def first_du_rest(m):
                dve.wait_ge(split_step, m * 4 + 2)
                dve.tensor_tensor(tmp0[:], tmp1[:], parts[:, 0, 1, :].rearrange("p (d t) -> p d t", d=2),
                                  ALU.subtract).then_inc(urest_done, 1)

            def first_du_last(m):
                dve.wait_ge(split_step, m * 4 + 4)
                dve.tensor_tensor(parts[:, 2, 1, :].rearrange("p (d t) -> p d t", d=2), tmp0[:],
                                  parts[:, 1, 1, :].rearrange("p (d t) -> p d t", d=2),
                                  ALU.subtract).then_inc(uparts_ready, 1)

            def read_out(o, m, i, odd):
                dve.wait_ge(out_ready, m + 1)
                if o == 0:
                    dve.tensor_copy(xrec[C * odd:C * odd + C, bass.ds(i * TOK, TOK)],
                                    pre[C * odd:C * odd + C, :]).then_inc(xrec_done, 1)
                else:
                    at = i * 2 * SEQS + (SEQS if odd else 0)
                    v = xrec[:].rearrange("p (r w) -> p r w", w=W)[:, :, bass.ds(at, SEQS)]
                    dve.tensor_tensor(v, v, pre[:, 0:SEQS * HALF].rearrange("p (s r) -> p r s", s=SEQS),
                                      ALU.add).then_inc(xrec_done, 1)

            def start(b, o, n0):
                if o == 0:
                    dve.wait_ge(final_done, b * 16)
                    for h in range(2):
                        r = slice(C * h, C * h + C)
                        dve.memset(xp[r, 0:PAD * S + PAD - h], 0.0)
                        at = (PAD + 1) * S - h
                        dve.memset(xp[r, at:at + (H - 1) * S].rearrange("p (r w) -> p r w", w=S)[:, :, 0:PAD], 0.0)
                        ins = dve.memset(xp[r, (H + PAD) * S - h:XP], 0.0)
                    ins.then_inc(pads_ready, 1)
                else:
                    dve.wait_ge(z_ready, b * PER_IMAGE + TILES)
                    dve.memset(xp[C:P, (H + PAD - 1) * S:(H + PAD) * S], 0.0).then_inc(pads_ready, 1)
                if o == 0:
                    dve.wait_ge(stored, b * 128)
                else:
                    dve.wait_ge(xrec_done, n0)
                for d in range(2):
                    read_conv(o, n0, d, start_bank(0, d))
                for d in range(2):
                    read_conv(o, n0 + 1, d, start_bank(1, d), True)
                first_u(n0)
                correction(n0)
                log1p(n0)
                make_delta(n0)
                make_du(n0, 0)
                delta_rest(n0)
                first_du_rest(n0)
                delta_last(n0)
                first_du_last(n0)
                mulb(n0, 0, True)

            def body(o, i, n, par, first, stage_a, stage_b):
                m, mpar = n + 1, 1 - par
                for s in range(UNITS):
                    if s < UNITS - 1:
                        mulb(n, s + 1, first)
                    elif stage_b:
                        mulb(m, 0, False)
                    if stage_b:
                        if s == 6:
                            log1p(m)
                        if s == 7:
                            make_du(m, mpar)
                    if not first and s == 4:
                        gate(n - 1)
                    if not first and s == 6:
                        read_out(o, n - 1, i if par else i - 1, mpar)
                    scan(n, s)
                    if stage_b:
                        if s == 5:
                            correction(m)
                        if s == 6:
                            make_delta(m)
                        if s == 9:
                            delta_last(m)
                    if stage_a and s in (11, 12):
                        read_conv(o, m + 1, s - 11)
                    if s == 13:
                        read_z(n, stage_b)

            def flush(b, o, n):
                gate(n)
                read_out(o, n, TILES // 2 - 1, 1)

            for b in phases(dve, start, body, flush):
                dve.wait_ge(xrec_done, b * PER_IMAGE + PER_IMAGE)
                for c in range(PIX // 512):
                    ins = dve.bn_stats(stats[:, c, :], xrec[:, c * 512:(c + 1) * 512])
                ins.then_inc(stat_done, 1)
                dve.wait_ge(stat_done, b * 10 + 1)
                dve.memset(st[:, 12:13], 0.0)
                dve.bn_aggr(st[:, 2:4], stats[:]).then_inc(stat_done, 1)
                dve.wait_ge(stat_done, b * 10 + 2)
                dve.tensor_copy(st[:, 0:1], st[:, 2:3])
                dve.scalar_tensor_tensor(st[:, 1:2], st[:, 2:3], st[:, 2:3], st[:, 3:4], ALU.mult,
                                         ALU.add).then_inc(stat_done, 1)
                dve.wait_ge(gm_ready, b + 1)
                dve.tensor_copy(st[:, 2:4], pre[:, 0:2]).then_inc(stat_done, 1)
                dve.wait_ge(stat_done, b * 10 + 4)
                dve.tensor_tensor(st[:, 4:5], st[:, 2:3], st[:, 2:3], ALU.mult).then_inc(stat_done, 1)
                dve.wait_ge(stat_done, b * 10 + 5)
                dve.tensor_tensor(st[:, 11:12], st[:, 3:4], st[:, 4:5], ALU.subtract).then_inc(stat_done, 1)
                dve.wait_ge(stat_done, b * 10 + 6)
                dve.tensor_scalar(st[:, 5:6], st[:, 11:12], 0.0, GN_EPS, ALU.max, ALU.add).then_inc(stat_done, 1)
                dve.wait_ge(rstd_step, b * 2 + 2)
                dve.tensor_tensor(st[:, 8:9], st[:, 7:8], gn_s[:, 0:1], ALU.mult).then_inc(stat_done, 1)
                dve.wait_ge(stat_done, b * 10 + 8)
                dve.tensor_tensor(st[:, 9:10], st[:, 2:3], st[:, 8:9], ALU.mult).then_inc(stat_done, 1)
                dve.wait_ge(stat_done, b * 10 + 9)
                dve.tensor_tensor(st[:, 10:11], gn_s[:, 1:2], st[:, 9:10], ALU.subtract).then_inc(stat_done, 1)
                dve.wait_ge(stat_done, b * 10 + 10)

                def norm(k):
                    v = chunk(xrec, ENDS_FIRST[k])
                    dve.tensor_scalar(v, v, st[:, 8:9], st[:, 10:11], ALU.mult, ALU.add).then_inc(norm_done, 1)

                def hold(k):
                    v = chunk(xrec, ENDS_FIRST[k])
                    dve.wait_ge(norm_done, b * 8 + k + 1)
                    dve.tensor_scalar(v, v, SILU_FLOOR, None, ALU.max).then_inc(floor_done, 1)

                def add_x(k):
                    c = ENDS_FIRST[k]
                    dve.wait_ge(act_done, b * 8 + k + 1)
                    dve.tensor_tensor(g_chunk(c), g_chunk(c), chunk(xrec, c).rearrange("p (r w) -> p r w", w=W),
                                      ALU.add).then_inc(g_done, 1)

                norm(0)
                for k in range(8):
                    if k < 7:
                        norm(k + 1)
                    hold(k)
                dve.wait_ge(g_loaded, b * 32 + 32)
                add_x(0)
                add_x(1)
                dve.wait_ge(g_done, b * 8 + 2)
                e0 = 1 + b * 18
                dve.tensor_tensor(g_all[0:C, 0, 1:1 + W], g_all[0:C, 1, 1:1 + W], g_all[0:C, 2, 1:1 + W], ALU.add)
                dve.tensor_tensor(g_all[C:P, GR - 1, 1:1 + W], g_all[C:P, GR - 2, 1:1 + W],
                                  g_all[C:P, GR - 3, 1:1 + W], ALU.add).then_inc(edge_done, 1)
                add_x(2)
                dve.wait_ge(edge_done, e0 + 1)
                dve.tensor_scalar(g_all[0:C, 0, 1:1 + W], g_all[0:C, 0, 1:1 + W], 0.5, None, ALU.mult)
                dve.tensor_scalar(g_all[C:P, GR - 1, 1:1 + W], g_all[C:P, GR - 1, 1:1 + W], 0.5, None,
                                  ALU.mult).then_inc(edge_done, 1)
                dve.wait_ge(edge_done, e0 + 2)
                dve.wait_ge(halo_loaded, b * 32 + 32)

                def final(c):
                    dve.wait_ge(mix_ready, b * 16 + c + 1)
                    dve.scalar_tensor_tensor(
                        xrec[:, c * 512:(c + 1) * 512].rearrange("p (r w) -> p r w", w=W),
                        pu[:, (c // 2) % 2, c % 2, :].rearrange("p (r w) -> p r w", w=W), gn_s[:, 2:3],
                        g_all[:, 1 + SEQS * c:1 + SEQS * c + SEQS, 1:1 + W], ALU.add, ALU.add).then_inc(final_done, 1)

                for j in range(8):
                    r0, r1 = (0 if j == 0 else CR * j + 1), (GR if j == 7 else CR * j + CR + 1)
                    if j > 0:
                        dve.wait_ge(g_done, b * 8 + min(j + 2, 8))
                    dve.tensor_tensor(g_all[:, r0:r1, 0], g_all[:, r0:r1, 1], g_all[:, r0:r1, 2], ALU.add)
                    dve.tensor_tensor(g_all[:, r0:r1, GW - 1], g_all[:, r0:r1, GW - 2], g_all[:, r0:r1, GW - 3],
                                      ALU.add).then_inc(edge_done, 1)
                    if 3 + j < 8:
                        add_x(3 + j)
                    dve.wait_ge(edge_done, e0 + 2 * j + 3)
                    dve.tensor_scalar(g_all[:, r0:r1, 0], g_all[:, r0:r1, 0], 0.5, None, ALU.mult)
                    dve.tensor_scalar(g_all[:, r0:r1, GW - 1], g_all[:, r0:r1, GW - 1], 0.5, None,
                                      ALU.mult).then_inc(edge_done, 1)
                    if j >= 2:
                        final(2 * j - 4)
                    dve.wait_ge(edge_done, e0 + 2 * j + 4)
                    dve.tensor_tensor(rows_all[:, r0:r1, :], g_all[:, r0:r1, 0:W], g_all[:, r0:r1, 1:1 + W],
                                      ALU.add).then_inc(rows_step, 1)
                    if j >= 2:
                        final(2 * j - 3)
                    dve.wait_ge(rows_step, b * 8 + j + 1)
                    dve.tensor_tensor(rows_all[:, r0:r1, :], rows_all[:, r0:r1, :], g_all[:, r0:r1, 2:2 + W],
                                      ALU.add).then_inc(rows_done, 1)
                for c in range(12, 16):
                    final(c)

        @block.gpsimd
        def _(pool):
            def mulc(n, unit, first):
                d = unit_parts(unit)[0]
                if unit % 8 == 0:
                    pool.wait_ge(bc_read, n * 4 + 2 * d + 2)
                pool.wait_ge(scan_done, n * UNITS + unit + 1)
                if first and unit == 2:
                    pool.wait_ge(u_ready, n + 2)
                if not (first and unit < 4) and unit % 2 == 0:
                    pool.wait_ge(hc_used, n * (UNITS // 2) + unit // 2 - 1)
                pool.tensor_tensor(hc[:, unit % 4], hid[:, unit % 4, :, :],
                                   Cb[:, d, :].unsqueeze(1).to_broadcast([P, 2, TOK]), ALU.mult).then_inc(mulc_done, 1)

            def silu_u(m, par, second=False):
                v, sigmoid = silu_scratch(second)
                pool.wait_ge(silu_step, m * 3 + 3)
                pool.tensor_tensor(u[:, par], v[:, :, :], sigmoid[:, :, :], ALU.mult).then_inc(u_ready, 1)

            def silu_z(m):
                pool.wait_ge(z_step, m * 3 + 3)
                pool.tensor_tensor(zs[:], tmp2[:, 0, :], tmp2[:, 1, :], ALU.mult).then_inc(zs_ready, 1)

            def delta_rest(m):
                pool.wait_ge(split_step, m * 4 + 1)
                pool.tensor_tensor(tmp2[:], delta[:], parts[:, 0, 0, :].rearrange("p (d t) -> p d t", d=2),
                                   ALU.subtract).then_inc(drest_done, 1)

            def du_rest(m):
                pool.wait_ge(split_step, m * 4 + 2)
                pool.tensor_tensor(tmp0[:], tmp1[:], parts[:, 0, 1, :].rearrange("p (d t) -> p d t", d=2),
                                   ALU.subtract).then_inc(urest_done, 1)

            def du_last(m):
                pool.wait_ge(split_step, m * 4 + 4)
                pool.wait_ge(dparts_ready, m + 1)
                pool.tensor_tensor(parts[:, 2, 1, :].rearrange("p (d t) -> p d t", d=2), tmp0[:],
                                   parts[:, 1, 1, :].rearrange("p (d t) -> p d t", d=2),
                                   ALU.subtract).then_inc(uparts_ready, 1)

            def start(b, o, n0):
                pool.wait_ge(u_ready, n0 + 1)
                silu_u(n0 + 1, 1, True)

            def body(o, i, n, par, first, stage_a, stage_b):
                for s in range(UNITS):
                    mulc(n, s, first)
                    if s == 1 and not first:
                        silu_z(n - 1)
                    if stage_b and s == 6:
                        delta_rest(n + 1)
                        du_rest(n + 1)
                    if stage_b and s == 8:
                        du_last(n + 1)
                    if stage_a and s == 14:
                        silu_u(n + 2, par)

            for b in phases(pool, start, body, lambda b, o, n: silu_z(n)):
                for k in range(8):
                    v = chunk(xrec, ENDS_FIRST[k])
                    pool.wait_ge(gate_step, b * 24 + 3 * k + 3)
                    pool.tensor_tensor(v, v, gate_buffer(k), ALU.mult).then_inc(act_done, 1)


def kernel(**inputs):
    import numpy as np
    import concourse.bacc as bacc
    from concourse.bass_utils import run_bass_kernel_spmd

    a = {k: np.asarray(v) for k, v in inputs.items()}

    def both(name, lay):
        return np.stack([lay(a[f"L0_conv_{o}_{name}"]) for o in ("row", "col")])

    di = a["L0_conv_row_D"].shape[0]
    c = a["x"].shape[1]
    p = np.arange(P)
    rows, m = np.arange(3 * 32), np.arange(P)
    sel = np.zeros((3 * 32, 4, P), np.float32)
    for q in range(4):
        sel[:, q, :] = (rows % 32)[:, None] == (8 * q + m // STATES)[None, :]
    statesum = np.zeros((P, 4, 32), np.float32)
    for j in range(4):
        statesum[:, j, :] = (8 * j + p // STATES)[:, None] == np.arange(32)[None, :]
    place = np.arange(di).reshape(4, 4, 8).transpose(1, 0, 2).reshape(-1)
    size = c // GN_GROUPS
    groupmean = ((p[:, None] % c) // size == (p[None, :] % c) // size).astype(np.float32) / (2 * size)
    ins = {
        "x": a["x"],
        "inT": both("in_w", lambda w: np.concatenate([w[:di], w[di:][place]]).T),
        "convT": both("conv_w", lambda w: w.reshape(di, TAPS).T.reshape(-1)),
        "xpT": both("xp_w", lambda w: w.T),
        "xpdt": both("xp_w", lambda w: w[:w.shape[0] - 2 * STATES]),
        "dtT": both("dt_w", lambda w: w.T),
        "alog": both("A_log", lambda w: w.reshape(-1, P).T),
        "chan": np.stack([both("conv_b", lambda w: w), both("dt_b", lambda w: w), both("D", lambda w: w)], -1),
        "outT": both("out_w", lambda w: w.T[place]),
        "gn": np.stack([a["L0_conv_gn_w"], a["L0_conv_gn_b"], a["L1_conv_conv_b"]], -1),
        "mixT": a["L1_conv_conv_w"].T,
        "eye": np.eye(P, dtype=np.float32)[place],
        "sel": sel.reshape(3 * 32, -1),
        "statesum": statesum.reshape(P, -1),
        "groupmean": groupmean,
    }
    nc = bacc.Bacc("TRN2", target_bir_lowering=False, num_devices=1)
    arrays, args = {}, []
    for name, v in ins.items():
        v = np.ascontiguousarray(v)
        arrays[f"in_{name}_dram"] = v
        args.append(nc.dram_tensor(f"in_{name}_dram", v.shape, mybir.dt.from_np(v.dtype), kind="ExternalInput").ap())
    args.append(nc.dram_tensor("out_dram", a["x"].shape, F32, kind="ExternalOutput").ap())
    build(nc, *args)
    r = run_bass_kernel_spmd(nc, [arrays], core_ids=[0])
    return r.results[0]["out_dram"]
```
